# Optimizing a Trainium2 kernel written in Bass

```python
import numpy as np
import jax
import jax.numpy as jnp

def _softmax(x, axis=-1):
    return jax.nn.softmax(x, axis=axis)

def _gelu(x):
    return jax.nn.gelu(x, approximate=True)

def _silu(x):
    return jax.nn.silu(x)

def _sigmoid(x):
    return jax.nn.sigmoid(x)

def _layernorm(x, axis=-1, eps=1e-05):
    m = jnp.mean(x, axis=axis, keepdims=True)
    v = jnp.var(x, axis=axis, keepdims=True)
    return (x - m) / jnp.sqrt(v + eps)

def _scatter_add(tgt, idx, src, axis=0):
    return tgt.at[idx].add(src)

def _segment_sum(src, seg, n):
    return jax.ops.segment_sum(src, seg, n)
kernel_name = 'mk_macaron_d1_jaxref_r8_d07b52'

def setup_inputs(seed: int=0):
    np.random.seed(seed)
    _w = jnp.asarray

    def _L0_attn_setup():
        import jax, jax.numpy as jnp
        import numpy as np
        import math
        DIM = 128
        NUM_HEADS = 16
        BATCH = 2
        SEQ = 256

        def _get_attention_slopes(n):

            def pow2_slopes(n):
                start = 2 ** (-2 ** (-(math.log2(n) - 3)))
                return [start * start ** i for i in range(n)]
            if math.log2(n).is_integer():
                return pow2_slopes(n)
            c = 2 ** math.floor(math.log2(n))
            return pow2_slopes(c) + _get_attention_slopes(2 * c)[0::2][:n - c]
        key = jax.random.key(seed)
        k1, k2, k3 = jax.random.split(key, 3)
        x = jax.random.normal(k1, (BATCH, SEQ, DIM), dtype=jnp.float32)
        w_qkv = jax.random.normal(k2, (DIM, 3 * DIM), dtype=jnp.float32) / np.sqrt(DIM)
        w_proj = jax.random.normal(k3, (DIM, DIM), dtype=jnp.float32) / np.sqrt(DIM)
        return {'x': x, 'w_qkv': w_qkv, 'w_proj': w_proj}
    _L0_attn_in = _L0_attn_setup()

    def _L0_ffn_setup():
        import jax, jax.numpy as jnp
        import numpy as np
        D_MODEL = 128
        HIDDEN = 256
        E_ROUTED = 14
        E_SHARED = 2
        TOP_K = 2
        EPS = 1e-09
        RMS_EPS = 1.1920929e-07

        def _ffn(xn, rw, W1, W2):
            ms = jnp.mean(xn * xn, axis=-1, keepdims=True)
            h = xn * jax.lax.rsqrt(ms + RMS_EPS) * rw
            return jax.nn.silu(h @ W1) @ W2
        key = jax.random.key(seed)
        ks = jax.random.split(key, 9)
        B, T = (2, 128)
        x = jax.random.normal(ks[0], (B, T, D_MODEL), dtype=jnp.float32)
        router_w = jax.random.normal(ks[1], (D_MODEL, E_ROUTED), dtype=jnp.float32) * 0.006
        rms_w = jnp.ones((E_ROUTED, D_MODEL), dtype=jnp.float32)
        w1 = jax.random.normal(ks[2], (E_ROUTED, D_MODEL, HIDDEN), dtype=jnp.float32) * 0.02
        w2 = jax.random.normal(ks[3], (E_ROUTED, HIDDEN, D_MODEL), dtype=jnp.float32) * 0.02
        rms_w_s = jnp.ones((E_SHARED, D_MODEL), dtype=jnp.float32)
        w1_s = jax.random.normal(ks[4], (E_SHARED, D_MODEL, HIDDEN), dtype=jnp.float32) * 0.02
        w2_s = jax.random.normal(ks[5], (E_SHARED, HIDDEN, D_MODEL), dtype=jnp.float32) * 0.02
        return {'x': x, 'router_w': router_w, 'rms_w': rms_w, 'w1': w1, 'w2': w2, 'rms_w_s': rms_w_s, 'w1_s': w1_s, 'w2_s': w2_s}
    _L0_ffn_in = _L0_ffn_setup()
    _d = {'L0_attn_x': _L0_attn_in['x'], 'L0_attn_w_qkv': _L0_attn_in['w_qkv'], 'L0_attn_w_proj': _L0_attn_in['w_proj'], 'L0_ffn_router_w': _L0_ffn_in['router_w'], 'L0_ffn_rms_w': _L0_ffn_in['rms_w'], 'L0_ffn_w1': _L0_ffn_in['w1'], 'L0_ffn_w2': _L0_ffn_in['w2'], 'L0_ffn_rms_w_s': _L0_ffn_in['rms_w_s'], 'L0_ffn_w1_s': _L0_ffn_in['w1_s'], 'L0_ffn_w2_s': _L0_ffn_in['w2_s']}
    _x0 = _d['L0_attn_x']
    _d['L0_attn_x'] = jax.random.normal(jax.random.fold_in(jax.random.key(seed), 1), (4, 1024, 128), dtype=_x0.dtype)
    del _x0
    return _d

def reference(L0_attn_x, L0_attn_w_qkv, L0_attn_w_proj, L0_ffn_router_w, L0_ffn_rms_w, L0_ffn_w1, L0_ffn_w2, L0_ffn_rms_w_s, L0_ffn_w1_s, L0_ffn_w2_s):

    def _L0_attn_ref(x, w_qkv, w_proj):
        import jax, jax.numpy as jnp
        import numpy as np
        import math
        DIM = 128
        NUM_HEADS = 16
        BATCH = 2
        SEQ = 256

        def _get_attention_slopes(n):

            def pow2_slopes(n):
                start = 2 ** (-2 ** (-(math.log2(n) - 3)))
                return [start * start ** i for i in range(n)]
            if math.log2(n).is_integer():
                return pow2_slopes(n)
            c = 2 ** math.floor(math.log2(n))
            return pow2_slopes(c) + _get_attention_slopes(2 * c)[0::2][:n - c]
        B, N, D = x.shape
        H = NUM_HEADS
        Dh = D // H
        qkv = x @ w_qkv
        q, k, v = jnp.split(qkv, 3, axis=-1)
        split_heads = lambda t: t.reshape(B, N, H, Dh).transpose(0, 2, 1, 3)
        q, k, v = (split_heads(q), split_heads(k), split_heads(v))
        scale = Dh ** (-0.5)
        att = jnp.einsum('bhnd,bhmd->bhnm', q, k) * scale
        slopes = jnp.asarray(_get_attention_slopes(H), dtype=att.dtype)
        pos_bias = slopes[None, :, None, None] * jnp.arange(N, dtype=att.dtype)[None, None, None, :]
        att = att + pos_bias
        big_neg = jnp.finfo(att.dtype).min
        causal = jnp.tril(jnp.ones((N, N), dtype=bool))[None, None]
        att = jnp.where(causal, att, big_neg)
        att = jax.nn.softmax(att, axis=-1)
        out = jnp.einsum('bhnm,bhmd->bhnd', att, v)
        out = out.transpose(0, 2, 1, 3).reshape(B, N, D)
        return out @ w_proj

    def _L0_ffn_ref(x, router_w, rms_w, w1, w2, rms_w_s, w1_s, w2_s):
        import jax, jax.numpy as jnp
        import numpy as np
        D_MODEL = 128
        HIDDEN = 256
        E_ROUTED = 14
        E_SHARED = 2
        TOP_K = 2
        EPS = 1e-09
        RMS_EPS = 1.1920929e-07

        def _ffn(xn, rw, W1, W2):
            ms = jnp.mean(xn * xn, axis=-1, keepdims=True)
            h = xn * jax.lax.rsqrt(ms + RMS_EPS) * rw
            return jax.nn.silu(h @ W1) @ W2
        B, T, D = x.shape
        N = B * T
        xf = x.reshape(N, D)
        gates = jax.nn.softmax(xf @ router_w, axis=-1)
        top_v, top_i = jax.lax.top_k(gates, TOP_K)
        masked = jnp.zeros_like(gates).at[jnp.arange(N)[:, None], top_i].set(top_v)
        masked = masked / (masked.sum(axis=-1, keepdims=True) + EPS)
        routed = jax.vmap(lambda rw_, W1_, W2_: _ffn(xf, rw_, W1_, W2_))(rms_w, w1, w2)
        routed_out = jnp.einsum('end,ne->nd', routed, masked)
        shared = jax.vmap(lambda rw_, W1_, W2_: _ffn(xf, rw_, W1_, W2_))(rms_w_s, w1_s, w2_s).sum(0)
        return (routed_out + shared).reshape(B, T, D)
    x = L0_attn_x
    x = x + 0.5 * _L0_ffn_ref(_layernorm(x, axis=-1), L0_ffn_router_w, L0_ffn_rms_w, L0_ffn_w1, L0_ffn_w2, L0_ffn_rms_w_s, L0_ffn_w1_s, L0_ffn_w2_s)
    x = x + _L0_attn_ref(_layernorm(x, axis=-1), L0_attn_w_qkv, L0_attn_w_proj)
    x = x + 0.5 * _L0_ffn_ref(_layernorm(x, axis=-1), L0_ffn_router_w, L0_ffn_rms_w, L0_ffn_w1, L0_ffn_w2, L0_ffn_rms_w_s, L0_ffn_w1_s, L0_ffn_w2_s)
    return x

_drawn_inputs = setup_inputs


def setup_inputs(seed=0):
    import zlib

    import numpy as np

    out = dict(_drawn_inputs(seed))
    spreads = {'L0_ffn_rms_w': (1.0, 0.6), 'L0_ffn_rms_w_s': (1.0, 0.6)}
    factors = {}
    for name, (base, spread) in spreads.items():
        noise = np.random.default_rng([zlib.crc32(name.encode()), seed]).standard_normal(out[name].shape)
        drawn = base * np.exp(spread * noise) if base else spread * noise
        out[name] = jnp.asarray(drawn.astype(out[name].dtype))
    for name, factor in factors.items():
        out[name] = (out[name] * factor).astype(out[name].dtype)
    return out
```

```python
import math
from contextlib import ExitStack

import concourse.bass as bass
from concourse import mybir
from concourse.alu_op_type import AluOpType as ALU

F32 = mybir.dt.float32
BF16 = mybir.dt.bfloat16
U32 = mybir.dt.uint32
ACT = mybir.ActivationFunctionType
AXX = mybir.AxisListType.X

P = 128
BATCH, SEQ, D = 4, 1024, 128
HEADS, DH = 16, 8
HID = 256
E_ROUTED, E_SHARED = 14, 2
EXPERTS = E_ROUTED + E_SHARED
LN_EPS, RMS_EPS, GATE_EPS = 1e-5, 1.1920929e-07, 1e-9

TILES = BATCH * SEQ // P
BT = SEQ // P
CT = 4
CHUNK = CT * P
CHUNKS = TILES // CT

HALVES = [(e, half) for e in [*range(E_ROUTED, EXPERTS), *range(E_ROUTED)] for half in range(2)]
NH = len(HALVES)
GROUPS = [(0, 2 * E_SHARED)] + [(2 * (E_SHARED + e), 2 * (E_SHARED + e) + 2) for e in range(E_ROUTED)]
NG = len(GROUPS)
RING = 4

GH = 4
UNITS = HEADS // GH
PARTS = 3
TERMS = PARTS * PARTS * DH
PASS1_ROWS = TERMS + PARTS
PASS2_ROWS = PASS1_ROWS + PARTS
HALF = 512
VW = DH + 1
MASKED = -1e30

STEPS = [(jt, max(HALF * ih, P * jt), HALF * (ih + 1) - max(HALF * ih, P * jt), ih)
         for ih in range(2) for jt in range(4 * (ih + 1))]
NS = len(STEPS)
LAST_OF_HALF = {0: 3, 1: NS - 1}


def first_pass_banks():
    banks = []
    for it in range(BT):
        if it >= 4:
            banks += [([(h, it, 0, HALF)], 0) for h in range(GH)]
        width = P * (it % 4 + 1)
        each = {1: 4, 2: 2, 3: 1, 4: 1}[it % 4 + 1]
        for h0 in range(0, GH, each):
            banks.append(([(h, it, HALF * (it // 4), width) for h in range(h0, h0 + each)], it // 4))
    return banks


BANKS = first_pass_banks()
NB = len(BANKS)
BANKS_IN = [4] * 9 + [NB - 36] + [0] * (NS - 10)
BANKS_AT = [sum(BANKS_IN[:s]) for s in range(NS + 1)]
assert BANKS_AT[NS] == NB

USES = []
for _g in range(UNITS):
    for _s in range(NS):
        if _g == 0 and 2 <= _s <= 5:
            USES.append((_g, _s, ("xn0", "xn1", "q0", "q1")[_s - 2]))
        if _g == 0 and _s == 6:
            USES.append((_g, _s, "k0"))
        if _g == 0 and 8 <= _s <= 10:
            USES.append((_g, _s, ("k1", "v0", "v1")[_s - 8]))
        if _s == 1 and _g:
            USES.append((_g, _s, "o1"))
        if _s == 7:
            USES.append((_g, _s, "o0"))
        if _s == 11:
            USES.append((_g, _s, "max"))
USES += [(UNITS, 0, n) for n in ("o1", "att0", "att1", "proj0", "proj1")]
USES_LAST = [u for u in USES if u[2][:-1] not in ("xn", "q", "k", "v") and u != (UNITS - 1, 11, "max")]
START = [(0, 0, n) for n in ("xn0", "xn1", "q0", "q1", "k0", "k1", "v0", "v1", "max")]


def build(nc, x, w_qkv, w_proj, router_w, rms_w, w1, w2, rms_w_s, w1_s, w2_s, alibi, out, phases=(1, 1, 1)):
    ctx = ExitStack()
    with ctx:
        def sb(name, shape, dt=F32):
            return ctx.enter_context(nc.sbuf_tensor(name, shape, dt))

        def sem(name):
            return ctx.enter_context(nc.semaphore(name))

        xs = sb("xs", [P, TILES, D])
        w1s = sb("w1s", [P, EXPERTS, HID])
        w2s = sb("w2s", [P, EXPERTS, 2, D])
        wr = sb("wr", [P, E_ROUTED])
        rms_rows = sb("rms_rows", [EXPERTS, D])
        rms_cols = sb("rms_cols", [P, EXPERTS])
        wqkv = sb("wqkv", [P, 3 * D])
        wproj = sb("wproj", [P, D])
        ident = sb("ident", [P, P])
        identb = sb("identb", [P, P], BF16)
        maskb = sb("maskb", [P, P], BF16)
        experts_row = sb("experts_row", [P, E_ROUTED])
        minus_half = sb("minus_half", [P, BT])
        plus_half = sb("plus_half", [P, BT])
        ln_eps = sb("ln_eps", [P, BT])
        one = sb("one", [P, 1])
        stats = sb("stats", [P, BT, 6])
        mv = sb("mv", [P, BT, 2])
        var_eps = sb("var_eps", [P, BT])
        rstd = sb("rstd", [P, BT])
        ms = sb("ms", [P, BT])
        rr = sb("rr", [P, BT])
        inv_rms = sb("inv_rms", [P, BT])
        xh = sb("xh", [P, CT, D])
        xT = [sb(f"xT{i}", [P, CHUNK]) for i in range(2)]
        work = sb("work", [P, 2 * RING, CHUNK])
        th = [work[:, i, :] for i in range(RING)]
        uu = [work[:, RING + i, :] for i in range(RING)]
        lg = sb("lg", [P, CT, E_ROUTED])
        mx8 = sb("mx8", [P, CT, 8])
        ix8 = sb("ix8", [P, CT, 8], U32)
        ixf = sb("ixf", [P, CT, 2])
        below = sb("below", [P, CT, E_ROUTED + 1])
        ex = sb("ex", [P, CT, E_ROUTED + 1])
        hot = sb("hot", [P, 2, CT, E_ROUTED])
        esum = sb("esum", [P, CT])
        den = sb("den", [P, CT])
        gates = [sb(f"gates{i}", [P, CT, E_ROUTED]) for i in range(2)]
        xn = sb("xn", [P, BT, D])
        xnT = sb("xnT", [P, SEQ])
        qf = sb("qf", [P, SEQ])
        kf = sb("kf", [P, SEQ])
        rest = sb("rest", [P, SEQ])
        qp = sb("qp", [P, PARTS, SEQ], BF16)
        kp = sb("kp", [P, PARTS, SEQ], BF16)
        vst = sb("vst", [P, BT, D])
        vaug = sb("vaug", [P, BT, HEADS, VW])
        qs = [sb(f"qs{g}", [PASS2_ROWS, GH, SEQ], BF16) for g in range(UNITS)]
        ks = [sb(f"ks{g}", [PASS2_ROWS, GH, SEQ], BF16) for g in range(UNITS)]
        pT = [[work[:, 4 * i + 2 * j:4 * i + 2 * j + 2, :] for j in range(2)] for i in range(2)]
        nmax = sb("nmax", [P, GH, BT])
        nmax1 = sb("nmax1", [P, GH, 4])
        mrest = sb("mrest", [GH * BT, P])
        mp = sb("mp", [GH * BT, PARTS, P], BF16)
        oT = [sb(f"oT{i}", [P, HALF]) for i in range(2)]
        rden = sb("rden", [P, 4, GH])
        att = sb("att", [P, BT, D])
        attT = sb("attT", [P, SEQ])
        al = rest
        ap = qp

        q_scr = nc.dram_tensor("q_scr", [5, HEADS, DH, SEQ], BF16, kind="Internal").ap()
        k_scr = nc.dram_tensor("k_scr", [PARTS, HEADS, DH, SEQ], BF16, kind="Internal").ap()
        a_scr = nc.dram_tensor("a_scr", [PARTS, HEADS, SEQ], BF16, kind="Internal").ap()
        m_scr = nc.dram_tensor("m_scr", [2, PARTS, GH, BT, P], BF16, kind="Internal").ap()

        banks = ctx.enter_context(nc.psum_tensor("banks", [P, 8, 512], F32))
        ps_h = [banks[:, i, :] for i in range(RING)]
        ps_y = [banks[:, 4 + i, :] for i in range(2)]
        ps_t = banks[:, 6, :]
        ps_l = banks[:, 7, :]
        ps_s = [banks[:, 2 * i:2 * i + 2, :] for i in range(2)]
        ps_1 = [banks[:, 4 + i, :] for i in range(2)]
        ps_o = banks[:, 6, :]
        ps_m = banks[:, 7, :]

        s_x = sem("x_loaded")
        s_w = sem("weights_loaded")
        s_al = sem("bias_loaded")
        s_c = sem("constants_made")
        s_rmsT = sem("rms_transposed")
        s_wready = sem("weights_ready")
        class Ffn:
            pass
        ffn = []
        for f in range(2):
            o = Ffn()
            o.mv = sem(f"f{f}_stats")
            o.rr = sem(f"f{f}_rstd")
            o.xh = sem(f"f{f}_normed")
            o.xt = sem(f"f{f}_transposed")
            o.xts = sem(f"f{f}_transposed_in_sbuf")
            o.lg = sem(f"f{f}_logits")
            o.lgs = sem(f"f{f}_logits_below_max")
            o.ex = sem(f"f{f}_exps")
            o.h = sem(f"f{f}_hidden")
            o.t = sem(f"f{f}_tanh")
            o.u = sem(f"f{f}_act_ready")
            o.used = sem(f"f{f}_act_used")
            o.acc = sem(f"f{f}_group_added")
            ffn.append(o)
        s_mv = sem("a_stats")
        s_rr = sem("a_rstd")
        s_xn = sem("a_normed")
        s_use = sem("a_shared_bank_filled")
        s_free = sem("a_shared_bank_read")
        s_parts = sem("a_parts_made")
        s_alp = sem("a_bias_parts_made")
        s_ones = sem("a_ones_set")
        s_alw = sem("a_bias_written")
        s_alr = sem("a_bias_rows")
        s_pw = sem("a_parts_written")
        s_rows = [sem(f"a_rows_loaded{g}") for g in range(UNITS)]
        s_mp = sem("a_max_parts")
        s_mw = sem("a_max_written")
        s_mrow = sem("a_max_rows")
        s_va = sem("a_values_ready")
        s_b1 = sem("a_first_pass_bank")
        s_red = sem("a_first_pass_reduced")
        s_s = sem("a_scores")
        s_e = sem("a_probs")
        s_pv = sem("a_outputs")
        s_ot = sem("a_output_in_sbuf")
        s_att = sem("a_att_ready")
        s_oz = sem("a_output_bank_zeroed")
        s_done = sem("result_ready")
        s_out = sem("result_written")

        block = ctx.enter_context(nc.Block())

        @block.sync
        def _(sp):
            sp.dma_start(xs[:, 0:CT, :], x[:, 0:CT, :]).then_inc(s_x, 16)
            sp.dma_start(xs[:, CT:TILES, :], x[:, CT:TILES, :]).then_inc(s_x, 16)
            for dst, src in ((rms_rows[0:E_ROUTED, :], rms_w), (rms_rows[E_ROUTED:EXPERTS, :], rms_w_s),
                             (wr[:, :], router_w),
                             (w1s[:, E_ROUTED:EXPERTS, :], w1_s.rearrange("e d f -> d e f")),
                             (w2s[:, E_ROUTED:EXPERTS, :, :], w2_s.rearrange("e (c p) d -> p e c d", p=P)),
                             (w1s[:, 0:E_ROUTED, :], w1.rearrange("e d f -> d e f")),
                             (w2s[:, 0:E_ROUTED, :, :], w2.rearrange("e (c p) d -> p e c d", p=P)),
                             (wqkv[:, :], w_qkv), (wproj[:, :], w_proj)):
                sp.dma_start(dst, src).then_inc(s_w, 16)
            sp.dma_start(al[0:HEADS, :], alibi).then_inc(s_al, 16)
            sp.wait_ge(s_alp, 1)
            sp.dma_start(a_scr.rearrange("c h n -> h c n"), ap[0:HEADS, :, :]).then_inc(s_alw, 16)
            sp.wait_ge(s_alw, 16)
            sp.wait_ge(s_ones, 1)
            for g in range(UNITS):
                sp.dma_start(ks[g][TERMS:PASS1_ROWS, :, :],
                             a_scr[:, g * GH:(g + 1) * GH, :]).then_inc(s_alr, 16)
            sp.wait_ge(s_alr, 16 * UNITS)

            def write_parts(b):
                sp.wait_ge(s_parts, 2 * b + 1)
                for c in range(5):
                    sp.dma_start(q_scr[c].rearrange("h d n -> (h d) n"), qp[:, c % PARTS, :]).then_inc(s_pw, 16)
                sp.wait_ge(s_parts, 2 * b + 2)
                for c in range(PARTS):
                    sp.dma_start(k_scr[c].rearrange("h d n -> (h d) n"), kp[:, c, :]).then_inc(s_pw, 16)
                sp.wait_ge(s_pw, 128 * b + 128)

            def load_rows(g):
                for a in range(PARTS):
                    for c in range(PARTS):
                        rows = slice((a * PARTS + c) * DH, (a * PARTS + c + 1) * DH)
                        sp.dma_start(qs[g][rows, :, :],
                                     q_scr[a + c, g * GH:(g + 1) * GH, :, :].rearrange("h d n -> d h n")
                                     ).then_inc(s_rows[g], 16)
                        sp.dma_start(ks[g][rows, :, :],
                                     k_scr[c, g * GH:(g + 1) * GH, :, :].rearrange("h d n -> d h n")
                                     ).then_inc(s_rows[g], 16)

            def max_rows(b, g):
                u = b * UNITS + g
                sp.wait_ge(s_mp, u + 1)
                sp.dma_start(m_scr[g % 2].rearrange("c h t p -> (h t) c p"), mp[:, :, :]).then_inc(s_mw, 16)
                sp.wait_ge(s_mw, 16 * u + 16)
                sp.dma_start(qs[g][PASS1_ROWS:PASS2_ROWS, :, :],
                             m_scr[g % 2].rearrange("c h t p -> c h (t p)")).then_inc(s_mrow, 16)

            def batch(b, last):
                for g in range(UNITS):
                    if g + 1 < UNITS:
                        max_rows(b, g + 1)
                    elif not last:
                        max_rows(b + 1, 0)
                    if last:
                        continue
                    if g == 0:
                        write_parts(b + 1)
                    sp.wait_ge(s_pv, 2 + (b * UNITS + g + 1) * NS)
                    load_rows(g)

            if phases[1]:
                write_parts(0)
                for g in range(UNITS):
                    load_rows(g)
                max_rows(0, 0)
                with sp.Fori(0, BATCH - 1) as b:
                    batch(b, False)
                batch(BATCH - 1, True)
            sp.wait_ge(s_done, 1)
            sp.dma_start(out, xs[:, :, :]).then_inc(s_out, 16)
            sp.wait_ge(s_out, 16)

        @block.gpsimd
        def _(pool):
            nc.gpsimd.memset(ident[:, :], 0.0)
            nc.gpsimd.memset(identb[:, :], 0.0)
            nc.gpsimd.memset(maskb[:, :], 0.0)
            nc.gpsimd.memset(minus_half[:, :], -0.5)
            nc.gpsimd.memset(plus_half[:, :], 0.5)
            nc.gpsimd.memset(ln_eps[:, :], LN_EPS)
            nc.gpsimd.memset(one[:, :], 1.0)
            nc.gpsimd.iota(experts_row[:, :], pattern=[[1, E_ROUTED]], base=0, channel_multiplier=0,
                           allow_small_or_imprecise_dtypes=True)
            pool.drain()
            for m in (ident, identb):
                nc.gpsimd.affine_select(out=m[:, :], in_=m[:, :], compare_op=ALU.not_equal, fill=1.0,
                                        base=0, pattern=[[-1, P]], channel_multiplier=1)
            nc.gpsimd.affine_select(out=maskb[:, :], in_=maskb[:, :], compare_op=ALU.is_ge, fill=MASKED,
                                    base=0, pattern=[[-1, P]], channel_multiplier=1)
            pool.drain().then_inc(s_c, 1)

            def powers(n, rms):
                w = slice(0, n)
                nc.gpsimd.tensor_tensor(var_eps[:, w], mv[:, w, 1], ln_eps[:, w], ALU.add)
                pool.drain()
                nc.gpsimd.tensor_tensor(rstd[:, w], var_eps[:, w], minus_half[:, w], ALU.pow)
                pool.drain()
                if not rms:
                    return
                nc.gpsimd.tensor_tensor(ms[:, w], mv[:, w, 1], rstd[:, w], ALU.mult)
                pool.drain()
                nc.gpsimd.tensor_tensor(ms[:, w], ms[:, w], rstd[:, w], ALU.mult)
                pool.drain()
                nc.gpsimd.tensor_scalar(ms[:, w], ms[:, w], RMS_EPS, None, ALU.add)
                pool.drain()
                nc.gpsimd.tensor_tensor(rr[:, w], ms[:, w], minus_half[:, w], ALU.pow)
                nc.gpsimd.tensor_tensor(inv_rms[:, w], ms[:, w], plus_half[:, w], ALU.pow)
                pool.drain()
                nc.gpsimd.tensor_tensor(rr[:, w], rr[:, w], rstd[:, w], ALU.mult)
                pool.drain()

            def ffn_norms(f):
                o = ffn[f]
                with pool.Fori(0, CHUNKS) as c:
                    pool.wait_ge(o.mv, c + 1)
                    powers(CT, True)
                    pool.drain().then_inc(o.rr, 1)

            def split(src, parts, tmp, n):
                nc.gpsimd.tensor_tensor(parts[:n, 0, :], src[:n, :], one[:n, :].to_broadcast([n, SEQ]), ALU.mult)
                pool.drain()
                nc.gpsimd.tensor_tensor(tmp[:n, :], src[:n, :], parts[:n, 0, :], ALU.subtract)
                pool.drain()
                nc.gpsimd.tensor_copy(parts[:n, 1, :], tmp[:n, :])
                pool.drain()
                nc.gpsimd.tensor_tensor(parts[:n, 2, :], tmp[:n, :], parts[:n, 1, :], ALU.subtract)

            def values(b):
                pool.wait_ge(s_pv, 2 + b * UNITS * NS)
                v = vst[:, :, :].rearrange("p t (h d) -> p (t h) d", d=DH)
                nc.gpsimd.tensor_tensor(vaug[:, :, :, 0:DH].rearrange("p t h d -> p (t h) d"), v,
                                        one[:, :].unsqueeze(2).to_broadcast([P, BT * HEADS, DH]),
                                        ALU.mult).then_inc(s_va, 1)

            def norm_and_parts(b, base, names):
                pool.wait_ge(s_mv, b + 1)
                powers(BT, False)
                pool.drain().then_inc(s_rr, 1)
                at = {n: i for i, (_, _, n) in enumerate(names)}
                pool.wait_ge(s_free, base + at["q1"] + 2)
                if not isinstance(b, int) or b:
                    pool.wait_ge(s_pw, 128 * b)
                split(qf, qp, rest, P)
                pool.drain().then_inc(s_parts, 1)
                pool.wait_ge(s_free, base + at["k1"] + 2)
                split(kf, kp, rest, P)
                pool.drain().then_inc(s_parts, 1)

            for g in range(UNITS):
                nc.gpsimd.memset(ks[g][:, :, :], 1.0)
                nc.gpsimd.memset(qs[g][:, :, :], 1.0)
            nc.gpsimd.memset(vaug[:, :, :, DH:VW], 1.0)
            pool.drain().then_inc(s_ones, 1)
            if phases[0]:
                ffn_norms(0)
            pool.wait_ge(s_al, 16)
            split(al, ap, kf, HEADS)
            pool.drain().then_inc(s_alp, 1)
            pool.wait_ge(s_alw, 16)
            if phases[1]:
                norm_and_parts(0, 0, START)
                pool.wait_ge(s_free, len(START))
                values(0)
                with pool.Fori(0, BATCH - 1) as b:
                    norm_and_parts(b + 1, len(START) + b * len(USES), USES)
                    pool.wait_ge(s_free, 1 + len(START) + (b + 1) * len(USES))
                    values(b + 1)
            if phases[2]:
                ffn_norms(1)

        @block.scalar
        def _(act):
            def run_ffn(f):
                o = ffn[f]

                def transposed(c, par):
                    act.wait_ge(o.xt, c + 1)
                    nc.scalar.activation(xT[par][:, :], ps_t, ACT.Copy).then_inc(o.xts, 1)

                def exps(c):
                    act.wait_ge(o.lgs, c + 1)
                    nc.scalar.activation(ex[:, :, :], below[:, :, :], ACT.Exp).then_inc(o.ex, 1)

                def chunk(c, par, last):
                    for k in range(NH):
                        act.wait_ge(o.h, c * NH + k + 1)
                        act.wait_ge(o.u, c * NH + k + 1)
                        nc.scalar.activation(th[k % RING], ps_h[k % RING], ACT.Tanh,
                                             scale=0.5).then_inc(o.t, 1)
                        if k == 13 and not last:
                            transposed(c + 1, 1 - par)
                        if k == 21 and not last:
                            exps(c + 1)

                transposed(0, 0)
                exps(0)
                with act.Fori(0, CHUNKS // 2 - 1) as i:
                    chunk(2 * i, 0, False)
                    chunk(2 * i + 1, 1, False)
                chunk(CHUNKS - 2, 0, False)
                chunk(CHUNKS - 1, 1, True)

            def use(b, base, i, name):
                if name[:-1] not in ("xn", "q", "k", "v", "att"):
                    return
                j = int(name[-1])
                cols = slice(j * 512, (j + 1) * 512)
                act.wait_ge(s_use, base + i + 1)
                if name[:-1] == "q" and b is not None:
                    act.wait_ge(s_parts, 2 * b + 2)
                if name == "v0" and b is not None:
                    act.wait_ge(s_va, b + 1)
                if name[:-1] == "xn":
                    ins = nc.scalar.activation(xnT[:, cols], ps_m, ACT.Copy)
                elif name[:-1] == "q":
                    ins = nc.scalar.activation(qf[:, cols], ps_m, ACT.Copy, scale=DH ** -0.5)
                elif name[:-1] == "k":
                    ins = nc.scalar.activation(kf[:, cols], ps_m, ACT.Copy)
                elif name[:-1] == "v":
                    ins = nc.scalar.activation(vst[:, 4 * j:4 * j + 4, :].rearrange("p t d -> p (t d)"),
                                               ps_m, ACT.Copy)
                else:
                    ins = nc.scalar.activation(attT[:, cols], ps_m, ACT.Copy)
                ins.then_inc(s_free, 1)

            def output(u, ih):
                act.wait_ge(s_pv, 2 + u * NS + LAST_OF_HALF[ih] + 1)
                nc.scalar.activation(oT[ih][:, :], ps_o, ACT.Copy).then_inc(s_ot, 1)

            def batch(b, last):
                base = len(START) + b * len(USES)
                uses = list(enumerate(USES_LAST if last else USES))
                for g in range(UNITS):
                    u = b * UNITS + g
                    for s, (jt, i0, w, ih) in enumerate(STEPS):
                        for pair in range(2):
                            n = u * 2 * NS + 2 * s + pair
                            act.wait_ge(s_s, n + 1)
                            if pair == 0:
                                act.wait_ge(s_pv, u * NS + s + 1)
                            nc.scalar.activation(pT[s % 2][pair][:, :, 0:w], ps_s[pair][:, :, 0:w],
                                                 ACT.Exp).then_inc(s_e, 1)
                        if s == LAST_OF_HALF[0] + 1:
                            output(u, 0)
                        if s == 0 and g:
                            output(u - 1, 1)
                        for i, (ug, us, name) in uses:
                            if (ug, us) == (g, s):
                                use(b, base, i, name)
                output(b * UNITS + UNITS - 1, 1)
                for i, (ug, us, name) in uses:
                    if ug == UNITS:
                        use(b, base, i, name)

            if phases[0]:
                run_ffn(0)
            if phases[1]:
                for i, (_, _, name) in enumerate(START):
                    use(None, 0, i, name)
                with act.Fori(0, BATCH - 1) as b:
                    batch(b, False)
                batch(BATCH - 1, True)
            if phases[2]:
                run_ffn(1)

        @block.vector
        def _(dve):
            dve.wait_ge(s_c, 1)
            for f in range(2):
                dve.drain().then_inc(ffn[f].u, RING)
                dve.drain().then_inc(ffn[f].used, RING)
                dve.drain().then_inc(ffn[f].acc, 2)
            dve.drain().then_inc(s_free, 1)
            for s in (s_red, s_e, s_pv):
                dve.drain().then_inc(s, 2)
            dve.drain().then_inc(s_ot, 1)
            dve.wait_ge(s_rmsT, 1)
            dve.wait_ge(s_w, 16 * 9)
            nc.vector.tensor_copy(rms_cols[:, :], ps_t[:, 0:EXPERTS])
            dve.drain()
            for e in range(EXPERTS):
                nc.vector.tensor_scalar(w1s[:, e, :], w1s[:, e, :], rms_cols[:, e:e + 1], None, ALU.mult)
            dve.drain().then_inc(s_wready, 1)
            dve.wait_ge(s_x, 32)

            def statistics(t0, n, signal):
                for t in range(n):
                    nc.vector.bn_stats(stats[:, t, :], xs[:, bass.ds(t0 + t, 1), :])
                dve.drain()
                for t in range(n):
                    nc.vector.bn_aggr(mv[:, t, :], stats[:, t, :])
                dve.drain().then_inc(signal, 1)

            def run_ffn(f):
                o = ffn[f]

                def norm(c):
                    statistics(c * CT, CT, o.mv)

                def normed(c, first):
                    dve.wait_ge(o.rr, c + 1)
                    if not first:
                        dve.wait_ge(o.xt, c)
                    for t in range(CT):
                        nc.vector.tensor_scalar(xh[:, t, :], xs[:, bass.ds(c * CT + t, 1), :],
                                                mv[:, t, 0:1], rr[:, t:t + 1], ALU.subtract, ALU.mult)
                    dve.drain().then_inc(o.xh, 1)

                def router(c):
                    dve.wait_ge(o.lg, c + 1)
                    nc.vector.tensor_tensor(
                        lg[:, :, :], ps_l.rearrange("p (t e) -> p t e", t=CT)[:, :, 0:E_ROUTED],
                        inv_rms[:, 0:CT].unsqueeze(2).to_broadcast([P, CT, E_ROUTED]), ALU.mult)
                    dve.drain()
                    for t in range(CT):
                        nc.vector.max(mx8[:, t, :], lg[:, t, :])
                    dve.drain()
                    for t in range(CT):
                        nc.vector.max_index(ix8[:, t, :], mx8[:, t, :], lg[:, t, :])
                    nc.vector.tensor_tensor(below[:, :, 0:E_ROUTED], lg[:, :, :],
                                            mx8[:, :, 0:1].to_broadcast([P, CT, E_ROUTED]), ALU.subtract)
                    nc.vector.tensor_tensor(below[:, :, E_ROUTED:E_ROUTED + 1], mx8[:, :, 1:2],
                                            mx8[:, :, 0:1], ALU.subtract)
                    dve.drain().then_inc(o.lgs, 1)
                    nc.vector.tensor_copy(ixf[:, :, :], ix8[:, :, 0:2])
                    dve.drain()
                    for j in range(2):
                        nc.vector.tensor_tensor(
                            hot[:, j, :, :], experts_row[:, :].unsqueeze(1).to_broadcast([P, CT, E_ROUTED]),
                            ixf[:, :, j:j + 1].to_broadcast([P, CT, E_ROUTED]), ALU.is_equal)
                    dve.drain()
                    nc.vector.tensor_tensor(hot[:, 0, :, :], hot[:, 0, :, :], hot[:, 1, :, :], ALU.add)

                def gate(c, par):
                    dve.wait_ge(o.ex, c + 1)
                    nc.vector.tensor_reduce(esum[:, :], ex[:, :, 0:E_ROUTED], axis=AXX, op=ALU.add)
                    dve.drain()
                    nc.vector.scalar_tensor_tensor(den[:, :], esum[:, :], GATE_EPS,
                                                   ex[:, :, E_ROUTED], ALU.mult, ALU.add)
                    dve.drain()
                    nc.vector.tensor_scalar(den[:, :], den[:, :], 1.0, 4.0, ALU.add, ALU.mult)
                    dve.drain()
                    nc.vector.reciprocal(den[:, :], den[:, :])
                    nc.vector.tensor_tensor(hot[:, 0, :, :], hot[:, 0, :, :], ex[:, :, 0:E_ROUTED], ALU.mult)
                    dve.drain()
                    nc.vector.tensor_tensor(gates[par][:, :, :], hot[:, 0, :, :],
                                            den[:, :].unsqueeze(2).to_broadcast([P, CT, E_ROUTED]), ALU.mult)
                    dve.drain()

                def add_group(c, par, gi):
                    dve.drain()
                    dve.wait_ge(o.used, RING + c * NH + GROUPS[gi][1])
                    bank = ps_y[(gi + par) % 2]
                    if gi == 0:
                        rows = xs[:, bass.ds(c * CT, CT), :]
                        nc.vector.scalar_tensor_tensor(rows, bank.rearrange("p (t d) -> p t d", t=CT), 0.25,
                                                       rows, ALU.mult, ALU.add).then_inc(o.acc, 1)
                        return
                    for t in range(CT):
                        rows = xs[:, bass.ds(c * CT + t, 1), :].rearrange("p t d -> p (t d)")
                        last = nc.vector.scalar_tensor_tensor(
                            rows, bank[:, t * D:(t + 1) * D], gates[par][:, t, gi - 1:gi], rows,
                            ALU.mult, ALU.add)
                    last.then_inc(o.acc, 1)

                def chunk(c, par, last):
                    done = 0
                    for k in range(NH):
                        dve.wait_ge(o.t, c * NH + k + 1)
                        dve.wait_ge(o.used, c * NH + k + 1)
                        nc.vector.scalar_tensor_tensor(uu[k % RING], th[k % RING], 1.0,
                                                       ps_h[k % RING], ALU.add, ALU.mult).then_inc(o.u, 1)
                        if done < NG and GROUPS[done][1] + 1 <= k:
                            add_group(c, par, done)
                            done += 1
                        if last:
                            continue
                        if k == 3:
                            norm(c + 1)
                        if k == 6:
                            normed(c + 1, False)
                        if k == 18:
                            router(c + 1)
                        if k == 24:
                            gate(c + 1, 1 - par)
                    while done < NG:
                        add_group(c, par, done)
                        done += 1

                norm(0)
                normed(0, True)
                router(0)
                gate(0, 0)
                with dve.Fori(0, CHUNKS // 2 - 1) as i:
                    chunk(2 * i, 0, False)
                    chunk(2 * i + 1, 1, False)
                chunk(CHUNKS - 2, 0, False)
                chunk(CHUNKS - 1, 1, True)
                dve.drain()

            def norm(b):
                statistics(b * BT, BT, s_mv)
                dve.wait_ge(s_rr, b + 1)
                for t in range(BT):
                    nc.vector.tensor_scalar(xn[:, t, :], xs[:, bass.ds(b * BT + t, 1), :],
                                            mv[:, t, 0:1], rstd[:, t:t + 1], ALU.subtract, ALU.mult)
                dve.drain().then_inc(s_xn, 1)

            def reduce_bank(u, n):
                pieces, half = BANKS[n]
                h0, it, _, w = pieces[0]
                dst = (nmax1[:, h0:h0 + len(pieces), it - 4] if half else nmax[:, h0:h0 + len(pieces), it])
                dve.wait_ge(s_b1, u * NB + n + 1)
                nc.vector.tensor_reduce(
                    dst, ps_1[n % 2][:, 0:len(pieces) * w].rearrange("p (h j) -> p h j", j=w),
                    axis=AXX, op=ALU.max, negate=True).then_inc(s_red, 1)

            def join_maxima(u):
                dve.drain()
                nc.vector.tensor_tensor(nmax[:, :, 4:8], nmax[:, :, 4:8], nmax1[:, :, :], ALU.min)
                dve.drain().then_inc(s_att, 1)

            def use(b, base, i, g, name, u_next):
                if name[:-1] not in ("o", "proj") and name != "max":
                    return
                dve.wait_ge(s_use, base + i + 1)
                if name == "max":
                    if u_next is not None:
                        dve.wait_ge(s_mw, 16 * u_next)
                    m = ps_m[0:GH * BT, 0:P]
                    nc.vector.tensor_copy(mp[:, 0, :], m)
                    dve.drain()
                    nc.vector.tensor_tensor(mrest[:, :], m, mp[:, 0, :], ALU.subtract).then_inc(s_free, 1)
                    dve.drain()
                    nc.vector.tensor_copy(mp[:, 1, :], mrest[:, :])
                    dve.drain()
                    nc.vector.tensor_tensor(mp[:, 2, :], mrest[:, :], mp[:, 1, :], ALU.subtract
                                            ).then_inc(s_mp, 1)
                elif name[0] == "o":
                    ih = int(name[1])
                    gg = g if ih == 0 else g - 1
                    v = ps_m.rearrange("p (t h c) -> p t h c", t=4, h=GH)
                    nc.vector.reciprocal(rden[:, :, :], v[:, :, :, DH])
                    dve.drain()
                    nc.vector.tensor_tensor(
                        att[:, 4 * ih:4 * ih + 4, gg * GH * DH:(gg + 1) * GH * DH
                            ].rearrange("p t (h d) -> p t h d", d=DH),
                        v[:, :, :, 0:DH], rden[:, :, :].unsqueeze(3).to_broadcast([P, 4, GH, DH]),
                        ALU.mult).then_inc(s_free, 1)
                else:
                    rows = xs[:, bass.ds(b * BT + 4 * int(name[-1]), 4), :]
                    nc.vector.tensor_tensor(rows, ps_m.rearrange("p (t d) -> p t d", t=4), rows,
                                            ALU.add).then_inc(s_free, 1)

            def batch(b, last):
                base = len(START) + b * len(USES)
                uses = list(enumerate(USES_LAST if last else USES))
                if not last:
                    norm(b + 1)
                for g in range(UNITS):
                    u = b * UNITS + g
                    first_pass = not (last and g == UNITS - 1)
                    for s in range(NS):
                        for n in range(BANKS_AT[s], BANKS_AT[s + 1]) if first_pass else ():
                            reduce_bank(u + 1, n)
                        if BANKS_IN[s] and BANKS_AT[s + 1] == NB and first_pass:
                            join_maxima(u + 1)
                        for i, (ug, us, name) in uses:
                            if (ug, us) == (g, s):
                                use(b, base, i, g, name, u + 1)
                for i, (ug, us, name) in uses:
                    if ug == UNITS:
                        use(b, base, i, UNITS, name, None)

            if phases[0]:
                run_ffn(0)
            if phases[1]:
                nc.vector.memset(ps_o, 0.0).then_inc(s_oz, 1)
                norm(0)
                for n in range(NB):
                    reduce_bank(0, n)
                join_maxima(0)
                use(0, 0, len(START) - 1, 0, "max", None)
                with dve.Fori(0, BATCH - 1) as b:
                    batch(b, False)
                batch(BATCH - 1, True)
            if phases[2]:
                dve.drain()
                run_ffn(1)
            dve.drain().then_inc(s_done, 1)

        @block.tensor
        def _(pe):
            mm = nc.tensor.matmul
            pe.wait_ge(s_c, 1)
            pe.wait_ge(s_w, 16 * 9)
            nc.tensor.transpose(ps_t[:, 0:EXPERTS], rms_rows[:, :], ident[0:EXPERTS, 0:EXPERTS]
                                ).then_inc(s_rmsT, 1)
            pe.wait_ge(s_wready, 1)

            def run_ffn(f):
                o = ffn[f]

                def transposes(c):
                    pe.wait_ge(o.xh, c + 1)
                    for t in range(CT):
                        last = nc.tensor.transpose(ps_t[:, t * P:(t + 1) * P], xh[:, t, :], ident[:, :])
                    last.then_inc(o.xt, 1)

                def logits(c, par):
                    pe.wait_ge(o.xts, c + 1)
                    for t in range(CT):
                        last = mm(ps_l[:, t * P:t * P + E_ROUTED], xT[par][:, t * P:(t + 1) * P],
                                  wr[:, :], start=True, stop=True)
                    last.then_inc(o.lg, 1)

                def hidden(c, par, k):
                    e, half = HALVES[k]
                    pe.wait_ge(o.u, c * NH + k + 1)
                    mm(ps_h[k % RING], w1s[:, e, half * P:(half + 1) * P], xT[par][:, :],
                       start=True, stop=True).then_inc(o.h, 1)

                def product(c, par, k):
                    e, half = HALVES[k]
                    gi = next(i for i, (a, z) in enumerate(GROUPS) if a <= k < z)
                    if k == GROUPS[gi][0]:
                        pe.wait_ge(o.acc, c * NG + gi + 1)
                    pe.wait_ge(o.u, RING + c * NH + k + 1)
                    for t in range(CT):
                        last = mm(ps_y[(gi + par) % 2][:, t * D:(t + 1) * D],
                                  uu[k % RING][:, t * P:(t + 1) * P], w2s[:, e, half, :],
                                  start=(k == GROUPS[gi][0] and t == 0), stop=(k == GROUPS[gi][1] - 1),
                                  skip_group_check=True)
                    last.then_inc(o.used, 1)

                def chunk(c, par, last):
                    for k in range(NH):
                        if k + 2 < NH:
                            hidden(c, par, k + 2)
                        if k == 12 and not last:
                            transposes(c + 1)
                        if k == 16 and not last:
                            logits(c + 1, 1 - par)
                        product(c, par, k)
                        if k >= NH - 2 and not last:
                            hidden(c + 1, 1 - par, k + 2 - NH)

                transposes(0)
                logits(0, 0)
                hidden(0, 0, 0)
                hidden(0, 0, 1)
                with pe.Fori(0, CHUNKS // 2 - 1) as i:
                    chunk(2 * i, 0, False)
                    chunk(2 * i + 1, 1, False)
                chunk(CHUNKS - 2, 0, False)
                chunk(CHUNKS - 1, 1, True)

            def first_pass(u, b, g, n):
                pieces, half = BANKS[n]
                if n == 0:
                    pe.wait_ge(s_rows[g], 16 * 18 * (b + 1))
                pe.wait_ge(s_red, u * NB + n + 1)
                for j, (h, it, j0, w) in enumerate(pieces):
                    dst = ps_1[n % 2][:, j * w:(j + 1) * w]
                    diagonal = j0 + w == (it + 1) * P
                    last = mm(dst, qs[g][0:PASS1_ROWS, h, it * P:(it + 1) * P],
                              ks[g][0:PASS1_ROWS, h, j0:j0 + w], start=True, stop=not diagonal)
                    if diagonal:
                        last = mm(dst[:, w - P:w], identb[:, :], maskb[:, :], start=False, stop=True)
                last.then_inc(s_b1, 1)

            def scores(u, g, s, pair):
                jt, i0, w, ih = STEPS[s]
                pe.wait_ge(s_e, u * 2 * NS + 2 * s + pair + 1)
                for j in range(2):
                    h = 2 * pair + j
                    diagonal = i0 == jt * P
                    last = mm(ps_s[pair][:, j, 0:w], ks[g][:, h, jt * P:(jt + 1) * P],
                              qs[g][:, h, i0:i0 + w], start=True, stop=not diagonal)
                    if diagonal:
                        last = mm(ps_s[pair][:, j, 0:P], maskb[:, :], identb[:, :], start=False, stop=True)
                last.then_inc(s_s, 1)

            def weigh(u, b, g, s):
                jt, i0, w, ih = STEPS[s]
                if jt == 0:
                    pe.wait_ge(s_ot, 2 * u + ih + 1)
                if s == 0 and g == 0:
                    pe.wait_ge(s_va, b + 1)
                pe.wait_ge(s_e, 2 + u * 2 * NS + 2 * s + 2)
                for h in range(GH):
                    last = mm(ps_o[32 * h:32 * h + VW, i0 - HALF * ih:HALF],
                              vaug[:, jt, g * GH + h, :], pT[s % 2][h // 2][:, h % 2, 0:w],
                              start=(jt == 0), stop=(s == LAST_OF_HALF[ih]))
                last.then_inc(s_pv, 1)

            def use(b, base, i, name, u, maxima):
                kind, j = (name, 0) if name == "max" else (name[:-1], int(name[-1]))
                cols = slice(512 * j, 512 * (j + 1))
                if kind == "xn" and j == 0:
                    pe.wait_ge(s_xn, maxima)
                if kind == "max":
                    pe.wait_ge(s_att, maxima)
                if kind == "o":
                    pe.wait_ge(s_ot, 1 + 2 * u + j + 1)
                pe.wait_ge(s_free, base + i + 1)
                if kind in ("xn", "att"):
                    src = xn if kind == "xn" else att
                    for t in range(4):
                        last = nc.tensor.transpose(ps_m[:, t * P:(t + 1) * P], src[:, 4 * j + t, :],
                                                   ident[:, :])
                elif kind in ("q", "k"):
                    at = 0 if kind == "q" else D
                    last = mm(ps_m, wqkv[:, at:at + D], xnT[:, cols], start=True, stop=True)
                elif kind in ("v", "proj"):
                    src, w = (xnT, wqkv[:, 2 * D:]) if kind == "v" else (attT, wproj[:, :])
                    for t in range(4):
                        last = mm(ps_m[:, t * D:(t + 1) * D], src[:, (4 * j + t) * P:(4 * j + t + 1) * P], w,
                                  start=True, stop=True)
                elif kind == "max":
                    last = nc.tensor.transpose(ps_m[0:GH * BT, 0:P],
                                               nmax[:, :, :].rearrange("p h t -> p (h t)"), ident[:, :])
                else:
                    for t in range(4):
                        last = nc.tensor.transpose(ps_m[:, t * P:(t + 1) * P], oT[j][:, t * P:(t + 1) * P],
                                                   ident[:, :])
                last.then_inc(s_use, 1)

            def batch(b, last):
                base = len(START) + b * len(USES)
                uses = list(enumerate(USES_LAST if last else USES))
                for g in range(UNITS):
                    u = b * UNITS + g
                    nb, ng = (b, g + 1) if g + 1 < UNITS else (b + 1, 0)
                    more = not (last and g == UNITS - 1)
                    pe.wait_ge(s_mrow, 16 * (u + 1))
                    scores(u, g, 0, 0)
                    scores(u, g, 0, 1)
                    for s in range(NS):
                        todo = list(range(BANKS_AT[s], BANKS_AT[s + 1])) if more else []
                        for n in todo[0:1]:
                            first_pass(u + 1, nb, ng, n)
                        if s + 1 < NS:
                            scores(u, g, s + 1, 0)
                        for n in todo[1:2]:
                            first_pass(u + 1, nb, ng, n)
                        if s + 1 < NS:
                            scores(u, g, s + 1, 1)
                        for n in todo[2:3]:
                            first_pass(u + 1, nb, ng, n)
                        for i, (ug, us, name) in uses:
                            if (ug, us) == (g, s):
                                use(b, base, i, name, u if name == "o0" else u - 1,
                                    b + 2 if name != "max" else u + 2)
                        weigh(u, b, g, s)
                        for n in todo[3:]:
                            first_pass(u + 1, nb, ng, n)
                for i, (ug, us, name) in uses:
                    if ug == UNITS:
                        use(b, base, i, name, b * UNITS + UNITS - 1, 0)

            if phases[0]:
                run_ffn(0)
            if phases[1]:
                pe.wait_ge(s_oz, 1)
                pe.wait_ge(s_alr, 16 * UNITS)
                pe.wait_ge(s_ones, 1)
                for i, (_, _, name) in enumerate(START[:-1]):
                    use(0, 0, i, name, 0, 1)
                for n in range(NB):
                    first_pass(0, 0, 0, n)
                use(0, 0, len(START) - 1, "max", 0, 1)
                with pe.Fori(0, BATCH - 1) as b:
                    batch(b, False)
                batch(BATCH - 1, True)
            if phases[2]:
                run_ffn(1)


def kernel(L0_attn_x, L0_attn_w_qkv, L0_attn_w_proj, L0_ffn_router_w, L0_ffn_rms_w, L0_ffn_w1,
           L0_ffn_w2, L0_ffn_rms_w_s, L0_ffn_w1_s, L0_ffn_w2_s):
    import numpy as np
    import concourse.bacc as bacc
    from concourse.bass_utils import run_bass_kernel_spmd

    start = 2.0 ** (-2.0 ** (-(math.log2(HEADS) - 3)))
    slopes = np.array([start * start ** i for i in range(HEADS)], np.float32)
    alibi = slopes[:, None] * np.arange(SEQ, dtype=np.float32)[None, :]

    nc = bacc.Bacc("TRN2", target_bir_lowering=False, num_devices=1)
    arrays, aps = {}, []
    for name, a in (("x", L0_attn_x), ("w_qkv", L0_attn_w_qkv), ("w_proj", L0_attn_w_proj),
                    ("router_w", L0_ffn_router_w), ("rms_w", L0_ffn_rms_w), ("w1", L0_ffn_w1),
                    ("w2", L0_ffn_w2), ("rms_w_s", L0_ffn_rms_w_s), ("w1_s", L0_ffn_w1_s),
                    ("w2_s", L0_ffn_w2_s), ("alibi", alibi)):
        a = np.ascontiguousarray(a)
        arrays[name] = a
        aps.append(nc.dram_tensor(name, a.shape, mybir.dt.from_np(a.dtype), kind="ExternalInput").ap())
    out = nc.dram_tensor("out", (BATCH, SEQ, D), F32, kind="ExternalOutput").ap()

    def by_tile(a):
        return a.rearrange("b (t p) d -> p (b t) d", p=P)

    build(nc, by_tile(aps[0]), *aps[1:], by_tile(out))
    r = run_bass_kernel_spmd(nc, [arrays], core_ids=[0])
    return r.results[0]["out"]
```

```python
import math
from contextlib import ExitStack

import concourse.bass as bass
import numpy as np
from concourse import mybir
from concourse.alu_op_type import AluOpType as ALU

F32 = mybir.dt.float32
BF16 = mybir.dt.bfloat16
U32 = mybir.dt.uint32
I32 = mybir.dt.int32
ACT = mybir.ActivationFunctionType
AXX = mybir.AxisListType.X

P = 128
BATCH, SEQ, D = 4, 1024, 128
HEADS, DH = 16, 8
HID = 256
E_ROUTED, E_SHARED = 14, 2
EXPERTS = E_ROUTED + E_SHARED
LN_EPS, RMS_EPS, GATE_EPS = 1e-5, 1.1920929e-07, 1e-9

TILES = BATCH * SEQ // P
BT = SEQ // P
CT = 4
CHUNK = CT * P
CHUNKS = TILES // CT

HALVES = [(e, half) for e in range(E_ROUTED, EXPERTS) for half in range(2)]
NH = len(HALVES)
SHARED = NH * CHUNKS
RING = 4

GROUPS = 2
GT = TILES // GROUPS
GC = CHUNKS // GROUPS
TOP_K = 2
RTILES = (TOP_K * GT * P + E_ROUTED * (P - 1)) // P
PAIRS = (RTILES + 1) // 2
RTILES = 2 * PAIRS
RS = 32

GH = 4
UNITS = HEADS // GH
PARTS = 3
TERMS = PARTS * PARTS * DH
PASS1_ROWS = TERMS + PARTS
PASS2_ROWS = PASS1_ROWS + PARTS
HALF = 512
VW = DH + 1
MASKED = -1e30

STEPS = [(jt, max(HALF * ih, P * jt), HALF * (ih + 1) - max(HALF * ih, P * jt), ih)
         for ih in range(2) for jt in range(4 * (ih + 1))]
NS = len(STEPS)
LAST_OF_HALF = {0: 3, 1: NS - 1}


def first_pass_banks():
    banks = []
    for it in range(BT):
        if it >= 4:
            banks += [([(h, it, 0, HALF)], 0) for h in range(GH)]
        width = P * (it % 4 + 1)
        each = {1: 4, 2: 2, 3: 1, 4: 1}[it % 4 + 1]
        for h0 in range(0, GH, each):
            banks.append(([(h, it, HALF * (it // 4), width) for h in range(h0, h0 + each)], it // 4))
    return banks


BANKS = first_pass_banks()
NB = len(BANKS)
BANKS_IN = [3, 3, 4, 4, 3, 3, 3, 2, 2, 3, 4, 4]
AHEAD = 8
EARLY = sum(BANKS_IN[AHEAD:])
assert sum(BANKS_IN) == NB


def banks_at(s):
    if s < AHEAD:
        first = EARLY + sum(BANKS_IN[:s])
        return range(first, first + BANKS_IN[s]), 1
    first = sum(BANKS_IN[AHEAD:s])
    return range(first, first + BANKS_IN[s]), 2


TURN = 6
FIRST_STEPS = [(0, 0, s) for s in range(TURN)]
BODY_STEPS = ([(0, 0, s) for s in range(TURN, NS)] + [(0, g, s) for g in range(1, UNITS) for s in range(NS)]
              + [(1, 0, s) for s in range(TURN)])
LAST_STEPS = BODY_STEPS[:-TURN]


def uses_at(g, s):
    at = []
    if s == 1:
        at.append("o1")
    if s == 7:
        at.append("o0")
    if s == 8:
        at.append("max")
    if g == 0 and 2 <= s <= 5:
        at.append(("att0", "att1", "proj0", "proj1")[s - 2])
    if g == 1 and s in (3, 4, 5, 6, 9, 10, 11):
        at.append({3: "xn0", 4: "xn1", 5: "q0", 6: "q1", 9: "k0", 10: "k1", 11: "v0"}[s])
    if g == 2 and s == 0:
        at.append("v1")
    return at


NEXT_BATCHS = ("xn0", "xn1", "q0", "q1", "k0", "k1", "v0", "v1")
START = [(0, 0, 0, n) for n in (*NEXT_BATCHS, "max")]
USES = [(db, g, s, n) for db, g, s in BODY_STEPS for n in uses_at(g, s)]
USES_LAST = [(db, g, s, n) for db, g, s in LAST_STEPS for n in uses_at(g, s)
             if n not in NEXT_BATCHS and (g, s, n) != (UNITS - 1, 8, "max")]
END = [(1, 0, 1, "o1"), (1, 0, 2, "att0"), (1, 0, 3, "att1"), (1, 0, 4, "proj0"), (1, 0, 5, "proj1")]


def numbered(uses, g, s, db=0):
    return [(i, n) for i, (d, ug, us, n) in enumerate(uses) if (d, ug, us) == (db, g, s)]



def build(nc, x, w_qkv, w_proj, router_w, rms_w, w1, w2, rms_w_s, w1_s, w2_s, alibi, out, phases=(1, 1, 1)):
    ctx = ExitStack()
    with ctx:
        def sb(name, shape, dt=F32):
            return ctx.enter_context(nc.sbuf_tensor(name, shape, dt))

        def sem(name):
            return ctx.enter_context(nc.semaphore(name))

        xs = sb("xs", [P, TILES, D])
        w1s = sb("w1s", [P, EXPERTS, HID])
        w2s = sb("w2s", [P, EXPERTS, 2, D])
        wr = sb("wr", [P, E_ROUTED])
        rms_rows = sb("rms_rows", [EXPERTS, D])
        rms_cols = sb("rms_cols", [P, EXPERTS])
        wqkv = sb("wqkv", [P, 3 * D])
        wproj = sb("wproj", [P, D])
        ident = sb("ident", [P, P])
        identb = sb("identb", [P, P], BF16)
        maskb = sb("maskb", [P, P], BF16)
        experts_row = sb("experts_row", [P, E_ROUTED])
        minus_half = sb("minus_half", [P, GT])
        plus_half = sb("plus_half", [P, GT])
        ln_eps = sb("ln_eps", [P, GT])
        one = sb("one", [P, 1])
        stats = sb("stats", [P, GT, 6])
        mv = sb("mv", [P, TILES, 2])
        var_eps = sb("var_eps", [P, GT])
        rstd = sb("rstd", [P, GT])
        ms = sb("ms", [P, GT])
        rr = sb("rr", [P, TILES])
        inv_rms = sb("inv_rms", [P, TILES])
        xT = [sb(f"xT{i}", [P, CHUNK]) for i in range(2)]
        work = sb("work", [P, 2 * RING, CHUNK])
        th = [work[:, i, :] for i in range(RING)]
        uu = [work[:, RING + i, :] for i in range(RING)]
        mx8 = sb("mx8", [P, GT, 8])
        ix8 = sb("ix8", [P, GT, 8], U32)
        ixf = sb("ixf", [P, GT, TOP_K])
        chosen = sb("chosen", [P, E_ROUTED, GT], BF16)
        posf = sb("posf", [P, TOP_K, GT])
        pos = [sb(f"pos{i}", [P, TOP_K, GT], U32) for i in range(GROUPS)]
        ntiles = sb("ntiles", [P, E_ROUTED])
        ends = sb("ends", [P, E_ROUTED])
        base_row = sb("base_row", [P, E_ROUTED])
        tile_ef = sb("tile_ef", [1, RTILES])
        tile_e = [sb(f"tile_e{i}", [1, RTILES], I32) for i in range(GROUPS)]
        esum = sb("esum", [P, GT])
        gates = [sb(f"gates{i}", [P, TOP_K, GT]) for i in range(GROUPS)]
        xld = [sb(f"xld{i}", [P, 2, D]) for i in range(2)]
        xTp = [sb(f"xTp{i}", [P, 2 * P]) for i in range(2)]
        w1c = [sb(f"w1c{i}", [P, 2, HID]) for i in range(2)]
        ysb = [sb(f"ysb{i}", [P, 2, D]) for i in range(2)]
        tri = sb("tri", [P, P], BF16)
        onesb = sb("onesb", [P, P], BF16)
        go_on = sb("go_on", [P, E_ROUTED, GT])
        ones_e = sb("ones_e", [P, E_ROUTED])
        hundreds = sb("hundreds", [P, GT])
        tiles_row = sb("tiles_row", [1, RTILES])
        region_a = sb("region_a", [P, 4, SEQ])
        region_b = sb("region_b", [P, 4, SEQ])
        taken = [0]

        def table(*dims, rows=P):
            at = taken[0]
            taken[0] += int(np.prod(dims))
            assert taken[0] <= 4 * SEQ
            flat = region_a[0:rows, :, :].rearrange("p a n -> p (a n)")[:, at:taken[0]]
            if len(dims) == 2:
                return flat.rearrange("p (a b) -> p a b", b=dims[1])
            return flat.rearrange("p (a b c) -> p a b c", b=dims[1], c=dims[2])

        lg = table(GT, E_ROUTED)
        below = table(GT, E_ROUTED + 1)
        ex = table(GT, E_ROUTED + 1)
        hot = table(TOP_K, GT, E_ROUTED)
        seen = table(E_ROUTED, GT)
        rank = table(E_ROUTED, GT)
        picked = table(TOP_K, GT, E_ROUTED)
        more_than = table(E_ROUTED, GT)
        ended = table(RTILES, E_ROUTED, rows=1)
        xn = region_a[:, 0, :].rearrange("p (t d) -> p t d", d=D)
        xnT = region_a[:, 1, :]
        qf = region_a[:, 2, :]
        kf = region_a[:, 3, :]
        att = region_b[:, 0, :].rearrange("p (t d) -> p t d", d=D)
        attT = region_b[:, 1, :]
        rest = region_b[:, 2, :]
        vst = region_b[:, 3, :].rearrange("p (t d) -> p t d", d=D)
        xh = region_b.rearrange("p a (t d) -> p (a t) d", d=D)
        got = [region.rearrange("p a (k t d) -> p (a k t) d", d=D, k=2).rearrange(
            "p (k t) d -> p k t d", k=TOP_K) for region in (region_a, region_b)]
        qp = sb("qp", [P, PARTS, SEQ], BF16)
        kp = sb("kp", [P, PARTS, SEQ], BF16)
        vaug = sb("vaug", [P, BT, HEADS, VW])
        qs = [sb(f"qs{g}", [PASS2_ROWS, GH, SEQ], BF16) for g in range(UNITS)]
        ks = [sb(f"ks{g}", [PASS2_ROWS, GH, SEQ], BF16) for g in range(UNITS)]
        pT = [[work[:, 4 * i + 2 * j:4 * i + 2 * j + 2, :] for j in range(2)] for i in range(2)]
        nmax = [sb(f"nmax{i}", [P, GH, BT]) for i in range(2)]
        nmax1 = sb("nmax_late_keys", [P, GH, 4])
        mrest = sb("mrest", [GH * BT, P])
        mp = sb("mp", [GH * BT, PARTS, P], BF16)
        oT = [sb(f"oT{i}", [P, HALF]) for i in range(2)]
        rden = sb("rden", [P, 4, GH])
        al = kf
        ap = qp

        sorted_x = [nc.dram_tensor(f"sorted_x{i}", [RTILES * P, D], F32, kind="Internal").ap()
                    for i in range(GROUPS)]
        FILLS = GROUPS * -(-RTILES * D // (2 * RING * CHUNK))
        sorted_y = [nc.dram_tensor(f"sorted_y{i}", [RTILES * P, D], F32, kind="Internal").ap()
                    for i in range(GROUPS)]
        q_scr = nc.dram_tensor("q_scr", [5, HEADS, DH, SEQ], BF16, kind="Internal").ap()
        k_scr = nc.dram_tensor("k_scr", [PARTS, HEADS, DH, SEQ], BF16, kind="Internal").ap()
        a_scr = nc.dram_tensor("a_scr", [PARTS, HEADS, SEQ], BF16, kind="Internal").ap()
        m_scr = nc.dram_tensor("m_scr", [2, PARTS, GH, BT, P], BF16, kind="Internal").ap()

        banks = ctx.enter_context(nc.psum_tensor("banks", [P, 8, 512], F32))
        ps_h = [banks[:, i, :] for i in range(RING)]
        ps_y = [banks[:, 4 + i, :] for i in range(2)]
        ps_r = banks[:, 5, :]
        ps_t = banks[:, 6, :]
        ps_l = banks[:, 7, :]
        ps_tp = [banks[:, 6 + i, :] for i in range(2)]
        ps_s = [banks[:, 2 * i:2 * i + 2, :] for i in range(2)]
        ps_1 = [banks[:, 4 + i, :] for i in range(2)]
        ps_o = banks[:, 6, :]
        ps_m = banks[:, 7, :]

        s_x = sem("x_loaded")
        s_zero = sem("zeros_made")
        s_fill = sem("sorted_filled")
        s_w = sem("weights_loaded")
        s_al = sem("bias_loaded")
        s_c = sem("constants_made")
        s_rmsT = sem("rms_transposed")
        s_wready = sem("weights_ready")
        class Ffn:
            pass
        ffn = []
        for f in range(2):
            o = Ffn()
            o.mv = sem(f"f{f}_stats")
            o.rr = sem(f"f{f}_rstd")
            o.xh = sem(f"f{f}_normed")
            o.xt = sem(f"f{f}_transposed")
            o.xts = sem(f"f{f}_transposed_in_sbuf")
            o.lg = sem(f"f{f}_logits")
            o.lgs = sem(f"f{f}_logits_below_max")
            o.ex = sem(f"f{f}_exps")
            o.h = sem(f"f{f}_hidden")
            o.t = sem(f"f{f}_tanh")
            o.u = sem(f"f{f}_act_ready")
            o.used = sem(f"f{f}_act_used")
            o.acc = sem(f"f{f}_shared_added")
            o.cho = sem(f"f{f}_experts_chosen")
            o.cnt = sem(f"f{f}_ranks")
            o.pos = sem(f"f{f}_rows_known")
            o.sc = [sem(f"f{f}_scattered{i}") for i in range(GROUPS)]
            o.xl = [sem(f"f{f}_rows_in{i}") for i in range(2)]
            o.pt = sem(f"f{f}_pair_transposed")
            o.pe = sem(f"f{f}_pair_in_sbuf")
            o.w1 = sem(f"f{f}_pair_weights")
            o.ye = sem(f"f{f}_pair_out_in_sbuf")
            o.ys = [sem(f"f{f}_rows_out{i}") for i in range(2)]
            o.got = [sem(f"f{f}_gathered{i}") for i in range(GROUPS)]
            ffn.append(o)
        s_mv = sem("a_stats")
        s_rr = sem("a_rstd")
        s_xn = sem("a_normed")
        s_use = sem("a_shared_bank_filled")
        s_free = sem("a_shared_bank_read")
        s_parts = sem("a_parts_made")
        s_alp = sem("a_bias_parts_made")
        s_ones = sem("a_ones_set")
        s_alw = sem("a_bias_written")
        s_alr = sem("a_bias_rows")
        s_pw = sem("a_parts_written")
        s_rows = [sem(f"a_rows_loaded{g}") for g in range(UNITS)]
        s_mp = sem("a_max_parts")
        s_mw = sem("a_max_written")
        s_mrow = sem("a_max_rows")
        s_va = sem("a_values_ready")
        s_b1 = sem("a_first_pass_bank")
        s_red = sem("a_first_pass_reduced")
        s_s = sem("a_scores")
        s_e = sem("a_probs")
        s_pv = sem("a_outputs")
        s_ot = sem("a_output_in_sbuf")
        s_max = sem("a_maxima")
        s_oz = sem("a_output_bank_zeroed")
        s_done = sem("result_ready")
        s_out = sem("result_written")

        block = ctx.enter_context(nc.Block())

        @block.sync
        def _(sp):
            sp.dma_start(xs[:, 0:CT, :], x[:, 0:CT, :]).then_inc(s_x, 16)
            sp.dma_start(xs[:, CT:TILES, :], x[:, CT:TILES, :]).then_inc(s_x, 16)
            for dst, src in ((rms_rows[0:E_ROUTED, :], rms_w), (rms_rows[E_ROUTED:EXPERTS, :], rms_w_s),
                             (wr[:, :], router_w),
                             (w1s[:, E_ROUTED:EXPERTS, :], w1_s.rearrange("e d f -> d e f")),
                             (w2s[:, E_ROUTED:EXPERTS, :, :], w2_s.rearrange("e (c p) d -> p e c d", p=P)),
                             (w1s[:, 0:E_ROUTED, :], w1.rearrange("e d f -> d e f")),
                             (w2s[:, 0:E_ROUTED, :, :], w2.rearrange("e (c p) d -> p e c d", p=P)),
                             (wqkv[:, :], w_qkv), (wproj[:, :], w_proj)):
                sp.dma_start(dst, src).then_inc(s_w, 16)
            sp.dma_start(al[0:HEADS, :], alibi).then_inc(s_al, 16)
            sp.wait_ge(s_zero, 1)
            for i in range(GROUPS):
                rows = sorted_x[i].rearrange("(t p) d -> p t d", p=P)
                for at in range(0, RTILES, 2 * RING * CHUNK // D):
                    n = min(2 * RING * CHUNK // D, RTILES - at)
                    sp.dma_start(rows[:, at:at + n, :],
                                 work.rearrange("p a (t d) -> p (a t) d", d=D)[:, 0:n, :]).then_inc(s_fill, 16)
            sp.wait_ge(s_alp, 1)
            sp.dma_start(a_scr.rearrange("c h n -> h c n"), ap[0:HEADS, :, :]).then_inc(s_alw, 16)
            sp.wait_ge(s_alw, 16)
            sp.wait_ge(s_ones, 1)
            for g in range(UNITS):
                sp.dma_start(ks[g][TERMS:PASS1_ROWS, :, :],
                             a_scr[:, g * GH:(g + 1) * GH, :]).then_inc(s_alr, 16)
            sp.wait_ge(s_alr, 16 * UNITS)

            def write_parts(b):
                sp.wait_ge(s_parts, 2 * b + 1)
                for c in range(5):
                    sp.dma_start(q_scr[c].rearrange("h d n -> (h d) n"), qp[:, c % PARTS, :]).then_inc(s_pw, 16)
                sp.wait_ge(s_parts, 2 * b + 2)
                for c in range(PARTS):
                    sp.dma_start(k_scr[c].rearrange("h d n -> (h d) n"), kp[:, c, :]).then_inc(s_pw, 16)
                sp.wait_ge(s_pw, 128 * b + 128)

            def load_rows(g):
                for a in range(PARTS):
                    for c in range(PARTS):
                        rows = slice((a * PARTS + c) * DH, (a * PARTS + c + 1) * DH)
                        sp.dma_start(qs[g][rows, :, :],
                                     q_scr[a + c, g * GH:(g + 1) * GH, :, :].rearrange("h d n -> d h n")
                                     ).then_inc(s_rows[g], 16)
                        sp.dma_start(ks[g][rows, :, :],
                                     k_scr[c, g * GH:(g + 1) * GH, :, :].rearrange("h d n -> d h n")
                                     ).then_inc(s_rows[g], 16)

            def max_rows(b, g):
                u = b * UNITS + g
                sp.wait_ge(s_mp, u + 1)
                sp.dma_start(m_scr[g % 2].rearrange("c h t p -> (h t) c p"), mp[:, :, :]).then_inc(s_mw, 16)
                sp.wait_ge(s_mw, 16 * u + 16)
                sp.dma_start(qs[g][PASS1_ROWS:PASS2_ROWS, :, :],
                             m_scr[g % 2].rearrange("c h t p -> c h (t p)")).then_inc(s_mrow, 16)

            def rows_of(b, g, before):
                sp.wait_ge(s_pv, 2 + (before * UNITS + g + 1) * NS)
                load_rows(g)

            def pairs(f):
                o = ffn[f]

                def load(r, i, k):
                    q0 = r * PAIRS + k
                    if not (isinstance(i, int) and q0 + 2 * i < 2):
                        sp.wait_ge(o.pt, 2 * i + q0 - 1)
                    rows = sorted_x[r].rearrange("(j t p) d -> j p t d", p=P, t=2)
                    sp.dma_start(xld[q0 % 2][:, :, :], rows[bass.ds(2 * i + k, 1)].rearrange(
                        "j p t d -> (j p) t d")).then_inc(o.xl[q0 % 2], 16)

                for r in range(GROUPS):
                    sp.wait_ge(o.sc[r], 16 * TOP_K * GT)
                    load(r, 0, 0)
                    load(r, 0, 1)
                    with sp.Fori(0, (PAIRS - 3) // 2) as i:
                        for k in range(2):
                            load(r, i, k + 2)
                    load(r, 0, PAIRS - 1)

            if phases[0]:
                pairs(0)
            if phases[1]:
                write_parts(0)
                for g in range(UNITS):
                    load_rows(g)
                max_rows(0, 0)
                with sp.Fori(0, BATCH - 1) as b:
                    max_rows(b, 1)
                    max_rows(b, 2)
                    write_parts(b + 1)
                    rows_of(b + 1, 0, b)
                    rows_of(b + 1, 1, b)
                    max_rows(b, 3)
                    rows_of(b + 1, 2, b)
                    max_rows(b + 1, 0)
                    rows_of(b + 1, 3, b)
                for g in range(1, UNITS):
                    max_rows(BATCH - 1, g)
            if phases[2]:
                pairs(1)
            sp.wait_ge(s_done, 1)
            sp.dma_start(out, xs[:, :, :]).then_inc(s_out, 16)
            sp.wait_ge(s_out, 16)

        @block.gpsimd
        def _(pool):
            nc.gpsimd.memset(ident[:, :], 0.0)
            nc.gpsimd.memset(identb[:, :], 0.0)
            nc.gpsimd.memset(maskb[:, :], 0.0)
            nc.gpsimd.memset(minus_half[:, :], -0.5)
            nc.gpsimd.memset(plus_half[:, :], 0.5)
            nc.gpsimd.memset(ln_eps[:, :], LN_EPS)
            nc.gpsimd.memset(one[:, :], 1.0)
            nc.gpsimd.memset(tri[:, :], 1.0)
            nc.gpsimd.memset(onesb[:, :], 1.0)
            nc.gpsimd.memset(ones_e[:, :], 1.0)
            nc.gpsimd.memset(go_on[:, :, :], 1.0)
            nc.gpsimd.iota(experts_row[:, :], pattern=[[1, E_ROUTED]], base=0, channel_multiplier=0,
                           allow_small_or_imprecise_dtypes=True)
            nc.gpsimd.iota(hundreds[:, :], pattern=[[P, GT]], base=0, channel_multiplier=0,
                           allow_small_or_imprecise_dtypes=True)
            nc.gpsimd.iota(tiles_row[:, :], pattern=[[1, RTILES]], base=0, channel_multiplier=0,
                           allow_small_or_imprecise_dtypes=True)
            pool.drain()
            for m in (ident, identb):
                nc.gpsimd.affine_select(out=m[:, :], in_=m[:, :], compare_op=ALU.not_equal, fill=1.0,
                                        base=0, pattern=[[-1, P]], channel_multiplier=1)
            nc.gpsimd.affine_select(out=tri[:, :], in_=tri[:, :], compare_op=ALU.is_gt, fill=0.0,
                                    base=0, pattern=[[1, P]], channel_multiplier=-1)
            nc.gpsimd.memset(go_on[:, :, 0:1], 0.0)
            nc.gpsimd.affine_select(out=maskb[:, :], in_=maskb[:, :], compare_op=ALU.is_ge, fill=MASKED,
                                    base=0, pattern=[[-1, P]], channel_multiplier=1)
            pool.drain().then_inc(s_c, 1)

            def powers(t0, n, rms):
                v = slice(t0, t0 + n)
                w = slice(0, n)
                nc.gpsimd.tensor_tensor(var_eps[:, w], mv[:, v, 1], ln_eps[:, w], ALU.add)
                pool.drain()
                nc.gpsimd.tensor_tensor(rstd[:, w], var_eps[:, w], minus_half[:, w], ALU.pow)
                pool.drain()
                if not rms:
                    return
                nc.gpsimd.tensor_tensor(ms[:, w], mv[:, v, 1], rstd[:, w], ALU.mult)
                pool.drain()
                nc.gpsimd.tensor_tensor(ms[:, w], ms[:, w], rstd[:, w], ALU.mult)
                pool.drain()
                nc.gpsimd.tensor_scalar(ms[:, w], ms[:, w], RMS_EPS, None, ALU.add)
                pool.drain()
                nc.gpsimd.tensor_tensor(rr[:, v], ms[:, w], minus_half[:, w], ALU.pow)
                nc.gpsimd.tensor_tensor(inv_rms[:, v], ms[:, w], plus_half[:, w], ALU.pow)
                pool.drain()
                nc.gpsimd.tensor_tensor(rr[:, v], rr[:, v], rstd[:, w], ALU.mult)
                pool.drain()

            def ffn_norms(f):
                o = ffn[f]
                for r in range(GROUPS):
                    pool.wait_ge(o.mv, r + 1)
                    powers(r * GT, GT, True)
                    pool.drain().then_inc(o.rr, 1)

            def route(f):
                o = ffn[f]
                for r in range(GROUPS):
                    pool.wait_ge(o.pos, r + 1)
                    pool.wait_ge(s_fill, 16 * FILLS)
                    for t in range(GT):
                        for k in range(TOP_K):
                            nc.gpsimd.indirect_dma_start(
                                out=sorted_x[r], out_offset=bass.IndirectOffsetOnAxis(ap=pos[r][:, k, t:t + 1], axis=0),
                                in_=xh[:, r * GT + t, :], in_offset=None).then_inc(o.sc[r], 16)
                for r in range(GROUPS):
                    for i in range(2):
                        pool.wait_ge(o.ys[i], 16 + 16 * sum(q % 2 == i for q in range((r + 1) * PAIRS)))
                    if r == 1:
                        pool.wait_ge(o.sc[1], 16 * TOP_K * GT)
                    for t in range(GT):
                        for k in range(TOP_K):
                            nc.gpsimd.indirect_dma_start(
                                out=got[r][:, k, t, :], out_offset=None, in_=sorted_y[r],
                                in_offset=bass.IndirectOffsetOnAxis(ap=pos[r][:, k, t:t + 1], axis=0),
                                ).then_inc(o.got[r], 16)

            def split(src, parts, tmp, n):
                nc.gpsimd.tensor_tensor(parts[:n, 0, :], src[:n, :], one[:n, :].to_broadcast([n, SEQ]), ALU.mult)
                pool.drain()
                nc.gpsimd.tensor_tensor(tmp[:n, :], src[:n, :], parts[:n, 0, :], ALU.subtract)
                pool.drain()
                nc.gpsimd.tensor_copy(parts[:n, 1, :], tmp[:n, :])
                pool.drain()
                nc.gpsimd.tensor_tensor(parts[:n, 2, :], tmp[:n, :], parts[:n, 1, :], ALU.subtract)

            def values(b):
                v = vst[:, :, :].rearrange("p t (h d) -> p t h d", d=DH)
                for jt in range(BT):
                    if not isinstance(b, int):
                        pool.wait_ge(s_pv, 2 + b * UNITS * NS - (BT - 1 - jt))
                    nc.gpsimd.tensor_tensor(vaug[:, jt, :, 0:DH], v[:, jt, :, :],
                                            one[:, :].unsqueeze(2).to_broadcast([P, HEADS, DH]),
                                            ALU.mult).then_inc(s_va, 1)

            def norm_and_parts(b, base, names):
                pool.wait_ge(s_mv, b + 1)
                powers(0, BT, False)
                pool.drain().then_inc(s_rr, 1)
                at = {n: i for i, (_, _, _, n) in enumerate(names)}
                pool.wait_ge(s_free, base + at["q1"] + 2)
                if not isinstance(b, int) or b:
                    pool.wait_ge(s_pw, 128 * b)
                split(qf, qp, rest, P)
                pool.drain().then_inc(s_parts, 1)
                pool.wait_ge(s_free, base + at["k1"] + 2)
                split(kf, kp, rest, P)
                pool.drain().then_inc(s_parts, 1)

            if phases[0]:
                ffn_norms(0)
            pool.wait_ge(s_al, 16)
            split(al, ap, qf, HEADS)
            pool.drain().then_inc(s_alp, 1)
            for g in range(UNITS):
                nc.gpsimd.memset(ks[g][:, :, :], 1.0)
                nc.gpsimd.memset(qs[g][:, :, :], 1.0)
            nc.gpsimd.memset(vaug[:, :, :, DH:VW], 1.0)
            pool.drain().then_inc(s_ones, 1)
            if phases[0]:
                route(0)
            if phases[1]:
                norm_and_parts(0, 0, START)
                pool.wait_ge(s_free, 1 + len(START) - 1)
                values(0)
                with pool.Fori(0, BATCH - 1) as b:
                    norm_and_parts(b + 1, len(START) + b * len(USES), USES)
                    pool.wait_ge(s_free, 2 + len(START) + b * len(USES) + [u[3] for u in USES].index("v1"))
                    values(b + 1)
            if phases[2]:
                ffn_norms(1)
                route(1)

        @block.scalar
        def _(act):
            def run_ffn(f):
                o = ffn[f]

                def transposed(c):
                    act.wait_ge(o.xt, c + 1)
                    nc.scalar.activation(xT[c % 2][:, :], ps_t, ACT.Copy).then_inc(o.xts, 1)

                def exps(r):
                    act.wait_ge(o.lgs, r + 1)
                    nc.scalar.activation(ex[:, :, :], below[:, :, :], ACT.Exp).then_inc(o.ex, 1)

                transposed(0)
                for c in range(CHUNKS):
                    for k in range(NH):
                        n = c * NH + k
                        act.wait_ge(o.h, n + 1)
                        act.wait_ge(o.u, n + 1)
                        nc.scalar.activation(th[n % RING], ps_h[n % RING], ACT.Tanh,
                                             scale=0.5).then_inc(o.t, 1)
                        if k == 1 and c + 1 < CHUNKS:
                            transposed(c + 1)
                    if c == GC - 1:
                        exps(0)
                exps(1)

                def bring(r, i, k):
                    q0 = r * PAIRS + k
                    act.wait_ge(o.pt, 2 * i + q0 + 1)
                    act.wait_ge(o.h, SHARED + 2 * i + q0 - 1)
                    nc.scalar.activation(xTp[q0 % 2][:, :], ps_tp[q0 % 2][:, 0:2 * P],
                                         ACT.Copy).then_inc(o.pe, 1)

                def tanh(r, i, k):
                    q0 = r * PAIRS + k
                    act.wait_ge(o.h, SHARED + 2 * i + q0 + 1)
                    nc.scalar.activation(th[q0 % 2], ps_h[q0 % 2], ACT.Tanh, scale=0.5).then_inc(o.t, 1)

                def out_rows(r, i, k):
                    q0 = r * PAIRS + k
                    act.wait_ge(o.used, RING + SHARED + 2 * i + q0 + 1)
                    act.wait_ge(o.ys[q0 % 2], 16 * (i + q0 // 2 + 1))
                    nc.scalar.activation(ysb[q0 % 2].rearrange("p t d -> p (t d)"),
                                         ps_y[q0 % 2][:, 0:2 * D], ACT.Copy).then_inc(o.ye, 1)

                def store(r, i, k):
                    q0 = r * PAIRS + k
                    act.wait_ge(o.ye, 2 + 2 * i + q0 + 1)
                    rows = sorted_y[r].rearrange("(j t p) d -> j p t d", p=P, t=2)
                    act.dma_start(rows[bass.ds(2 * i + k, 1)].rearrange("j p t d -> (j p) t d"),
                                  ysb[q0 % 2][:, :, :]).then_inc(o.ys[q0 % 2], 16)

                for r in range(GROUPS):
                    bring(r, 0, 0)
                    bring(r, 0, 1)
                    tanh(r, 0, 0)
                    bring(r, 0, 2)
                    with act.Fori(0, (PAIRS - 3) // 2) as i:
                        for k in range(2):
                            tanh(r, i, k + 1)
                            out_rows(r, i, k)
                            bring(r, i, k + 3)
                            store(r, i, k)
                    for k in range(PAIRS - 3, PAIRS):
                        if k + 1 < PAIRS:
                            tanh(r, 0, k + 1)
                        out_rows(r, 0, k)
                        if k + 3 < PAIRS:
                            bring(r, 0, k + 3)
                        store(r, 0, k)

            def use(b, base, i, name):
                if name[:-1] not in ("xn", "q", "k", "v", "att"):
                    return
                j = int(name[-1])
                cols = slice(j * 512, (j + 1) * 512)
                act.wait_ge(s_use, base + i + 1)
                if name[:-1] == "q" and b is not None:
                    act.wait_ge(s_parts, 2 * b + 2)
                if name == "v0" and b is not None:
                    act.wait_ge(s_va, BT * b + BT)
                if name[:-1] == "xn":
                    ins = nc.scalar.activation(xnT[:, cols], ps_m, ACT.Copy)
                elif name[:-1] == "q":
                    ins = nc.scalar.activation(qf[:, cols], ps_m, ACT.Copy, scale=DH ** -0.5)
                elif name[:-1] == "k":
                    ins = nc.scalar.activation(kf[:, cols], ps_m, ACT.Copy)
                elif name[:-1] == "v":
                    ins = nc.scalar.activation(vst[:, 4 * j:4 * j + 4, :].rearrange("p t d -> p (t d)"),
                                               ps_m, ACT.Copy)
                else:
                    ins = nc.scalar.activation(attT[:, cols], ps_m, ACT.Copy)
                ins.then_inc(s_free, 1)

            def output(u, ih):
                act.wait_ge(s_pv, 2 + u * NS + LAST_OF_HALF[ih] + 1)
                nc.scalar.activation(oT[ih][:, :], ps_o, ACT.Copy).then_inc(s_ot, 1)

            def steps(b0, span, uses):
                base = len(START) + b0 * len(USES)
                for db, g, s in span:
                    b = b0 + db
                    u = b * UNITS + g
                    jt, i0, w, ih = STEPS[s]
                    for pair in range(2):
                        n = u * 2 * NS + 2 * s + pair
                        act.wait_ge(s_s, n + 1)
                        if pair == 0:
                            act.wait_ge(s_pv, u * NS + s + 1)
                        nc.scalar.activation(pT[s % 2][pair][:, :, 0:w], ps_s[pair][:, :, 0:w],
                                             ACT.Exp).then_inc(s_e, 1)
                    if s == LAST_OF_HALF[0] + 1:
                        output(u, 0)
                    if s == 0 and (g or not isinstance(b, int) or b):
                        output(u - 1, 1)
                    for i, name in numbered(uses, g, s, db):
                        use(b0, base, i, name)

            if phases[0]:
                run_ffn(0)
            if phases[1]:
                for i, (_, _, _, name) in enumerate(START):
                    use(None, 0, i, name)
                steps(0, FIRST_STEPS, [])
                with act.Fori(0, BATCH - 1) as b:
                    steps(b, BODY_STEPS, USES)
                steps(BATCH - 1, LAST_STEPS, USES_LAST)
                output(BATCH * UNITS - 1, 1)
                for i, (_, _, _, name) in enumerate(END):
                    use(BATCH - 1, len(START) + (BATCH - 1) * len(USES) + len(USES_LAST), i, name)
            if phases[2]:
                run_ffn(1)

        @block.vector
        def _(dve):
            nc.vector.memset(work[:, :, :], 0.0).then_inc(s_zero, 1)
            dve.wait_ge(s_c, 1)
            for f in range(2):
                dve.drain().then_inc(ffn[f].u, RING)
                dve.drain().then_inc(ffn[f].used, RING)
                dve.drain().then_inc(ffn[f].ye, 2)
                for i in range(2):
                    dve.drain().then_inc(ffn[f].ys[i], 16)
            dve.drain().then_inc(s_free, 1)
            for s in (s_red, s_e, s_pv):
                dve.drain().then_inc(s, 2)
            dve.drain().then_inc(s_ot, 1)
            dve.wait_ge(s_rmsT, 1)
            dve.wait_ge(s_w, 16 * 9)
            nc.vector.tensor_copy(rms_cols[:, :], ps_t[:, 0:EXPERTS])
            dve.drain()
            for e in range(EXPERTS):
                nc.vector.tensor_scalar(w1s[:, e, :], w1s[:, e, :], rms_cols[:, e:e + 1], None, ALU.mult)
            dve.drain().then_inc(s_wready, 1)
            dve.wait_ge(s_x, 32)
            dve.wait_ge(s_fill, 16 * FILLS)

            def statistics(t0, n, to):
                for t in range(n):
                    nc.vector.bn_stats(stats[:, t, :], xs[:, bass.ds(t0 + t, 1), :])
                dve.drain()
                for t in range(n):
                    nc.vector.bn_aggr(mv[:, to + t, :], stats[:, t, :])

            def run_ffn(f):
                o = ffn[f]

                def group_stats(r):
                    statistics(r * GT, GT, r * GT)
                    dve.drain().then_inc(o.mv, 1)

                def normed(c):
                    dve.wait_ge(o.rr, c // GC + 1)
                    for t in range(c * CT, (c + 1) * CT):
                        nc.vector.tensor_scalar(xh[:, t, :], xs[:, t, :], mv[:, t, 0:1], rr[:, t:t + 1],
                                                ALU.subtract, ALU.mult)
                    dve.drain().then_inc(o.xh, 1)

                def by_tile(a):
                    return a.rearrange("p e t -> p t e")

                def choose(r):
                    dve.wait_ge(o.lg, (r + 1) * GC)
                    inv = inv_rms[:, r * GT:(r + 1) * GT]
                    dve.wait_ge(s_alp, 1)
                    nc.vector.tensor_tensor(
                        lg[:, :, :], ps_l.rearrange("p (t e) -> p t e", t=GT)[:, :, 0:E_ROUTED],
                        inv.unsqueeze(2).to_broadcast([P, GT, E_ROUTED]), ALU.mult)
                    dve.drain()
                    for t in range(GT):
                        nc.vector.max(mx8[:, t, :], lg[:, t, :])
                    dve.drain()
                    nc.vector.tensor_tensor(below[:, :, 0:E_ROUTED], lg[:, :, :],
                                            mx8[:, :, 0:1].to_broadcast([P, GT, E_ROUTED]), ALU.subtract)
                    nc.vector.tensor_tensor(below[:, :, E_ROUTED:E_ROUTED + 1], mx8[:, :, 1:2],
                                            mx8[:, :, 0:1], ALU.subtract)
                    dve.drain().then_inc(o.lgs, 1)
                    for t in range(GT):
                        nc.vector.max_index(ix8[:, t, :], mx8[:, t, :], lg[:, t, :])
                    dve.drain()
                    nc.vector.tensor_copy(ixf[:, :, :], ix8[:, :, 0:TOP_K])
                    dve.drain()
                    for j in range(TOP_K):
                        nc.vector.tensor_tensor(
                            hot[:, j, :, :], experts_row[:, :].unsqueeze(1).to_broadcast([P, GT, E_ROUTED]),
                            ixf[:, :, j:j + 1].to_broadcast([P, GT, E_ROUTED]), ALU.is_equal)
                    dve.drain()
                    nc.vector.tensor_tensor(by_tile(chosen[:, :, :]), hot[:, 0, :, :], hot[:, 1, :, :], ALU.add)
                    dve.drain().then_inc(o.cho, 1)

                def place(r):
                    dve.wait_ge(o.cnt, r + 1)
                    of_tile = ps_r[:, 256:256 + E_ROUTED * GT]
                    before = ps_r[:, 0:E_ROUTED * GT]

                    def flat(a):
                        return a[:, :, :].rearrange("p e t -> p (e t)")

                    nc.vector.tensor_tensor_scan(flat(seen), flat(go_on), of_tile, 0.0, ALU.mult, ALU.add)
                    dve.drain()
                    nc.vector.tensor_tensor(flat(rank), flat(seen), of_tile, ALU.subtract)
                    nc.vector.tensor_tensor(
                        more_than[:, :, :], seen[:, :, GT - 1:GT].to_broadcast([P, E_ROUTED, GT]),
                        hundreds[:, :].unsqueeze(1).to_broadcast([P, E_ROUTED, GT]), ALU.is_gt)
                    dve.drain()
                    nc.vector.tensor_tensor(flat(rank), flat(rank), before, ALU.add)
                    nc.vector.tensor_reduce(ntiles[:, :], more_than[:, :, :], axis=AXX, op=ALU.add)
                    dve.drain()
                    nc.vector.tensor_tensor_scan(ends[:, :], ones_e[:, :], ntiles[:, :], 0.0, ALU.mult, ALU.add)
                    dve.drain()
                    nc.vector.tensor_tensor(base_row[:, :], ends[:, :], ntiles[:, :], ALU.subtract)
                    nc.vector.tensor_tensor(
                        ended[:, :, :], ends[0:1, :].unsqueeze(1).to_broadcast([1, RTILES, E_ROUTED]),
                        tiles_row[:, :].unsqueeze(2).to_broadcast([1, RTILES, E_ROUTED]), ALU.is_le)
                    dve.drain()
                    nc.vector.scalar_tensor_tensor(
                        rank[:, :, :], base_row[:, :].unsqueeze(2).to_broadcast([P, E_ROUTED, GT]), float(P),
                        rank[:, :, :], ALU.mult, ALU.add)
                    nc.vector.tensor_reduce(tile_ef[:, :], ended[:, :, :], axis=AXX, op=ALU.add)
                    dve.drain()
                    nc.vector.tensor_scalar(tile_e[r][:, :], tile_ef[:, :], float(E_ROUTED - 1), None, ALU.min)
                    for j in range(TOP_K):
                        nc.vector.tensor_tensor(picked[:, j, :, :], hot[:, j, :, :], by_tile(rank[:, :, :]),
                                                ALU.mult)
                    dve.drain()
                    nc.vector.tensor_reduce(posf[:, :, :], picked[:, :, :, :], axis=AXX, op=ALU.add)
                    dve.drain()
                    nc.vector.tensor_copy(pos[r][:, :, :], posf[:, :, :])
                    dve.drain().then_inc(o.pos, 1)
                    dve.wait_ge(o.ex, r + 1)
                    nc.vector.tensor_reduce(esum[:, :], ex[:, :, 0:E_ROUTED], axis=AXX, op=ALU.add)
                    dve.drain()
                    nc.vector.scalar_tensor_tensor(esum[:, :], esum[:, :], GATE_EPS,
                                                   ex[:, :, E_ROUTED], ALU.mult, ALU.add)
                    dve.drain()
                    nc.vector.tensor_scalar(esum[:, :], esum[:, :], 1.0, 4.0, ALU.add, ALU.mult)
                    dve.drain()
                    nc.vector.reciprocal(gates[r][:, 0, :], esum[:, :])
                    dve.drain()
                    nc.vector.tensor_tensor(gates[r][:, 1, :], gates[r][:, 0, :], ex[:, :, E_ROUTED], ALU.mult)

                def activations(n, slot):
                    dve.wait_ge(o.t, n + 1)
                    nc.vector.scalar_tensor_tensor(uu[slot], th[slot], 1.0, ps_h[slot],
                                                   ALU.add, ALU.mult).then_inc(o.u, 1)

                def add_shared(c):
                    dve.drain()
                    dve.wait_ge(o.used, RING + (c + 1) * NH)
                    rows = xs[:, c * CT:(c + 1) * CT, :]
                    nc.vector.scalar_tensor_tensor(rows, ps_y[0].rearrange("p (t d) -> p t d", t=CT), 0.25,
                                                   rows, ALU.mult, ALU.add).then_inc(o.acc, 1)

                group_stats(0)
                normed(0)
                for c in range(CHUNKS):
                    if c == GC - 1:
                        choose(0)
                    if c == GC:
                        place(0)
                    for k in range(NH):
                        n = c * NH + k
                        dve.wait_ge(o.used, n + 1)
                        activations(n, n % RING)
                        if k == 0 and c + 1 < CHUNKS:
                            normed(c + 1)
                        if k == 1 and c:
                            add_shared(c - 1)
                    if c == 0:
                        for r in range(1, GROUPS):
                            group_stats(r)
                add_shared(CHUNKS - 1)
                choose(1)
                place(1)

                def pair_weights(r, i, k):
                    q0 = r * PAIRS + k
                    dve.wait_ge(o.h, SHARED + 2 * i + q0 - 1)
                    for a in range(2):
                        e = dve.value_load(tile_e[r][0:1, bass.ds(2 * (2 * i + k) + a, 1)],
                                           min_val=0, max_val=E_ROUTED - 1)
                        last = nc.vector.tensor_copy(w1c[q0 % 2][:, a:a + 1, :], w1s[:, bass.ds(e, 1), :])
                    last.then_inc(o.w1, 1)

                def pair_activations(r, i, k):
                    q0 = r * PAIRS + k
                    dve.wait_ge(o.used, RING + SHARED + 2 * i + q0 - 1)
                    activations(SHARED + 2 * i + q0, q0 % 2)

                for r in range(GROUPS):
                    pair_weights(r, 0, 0)
                    pair_weights(r, 0, 1)
                    with dve.Fori(0, (PAIRS - 3) // 2) as i:
                        for k in range(2):
                            pair_activations(r, i, k)
                            pair_weights(r, i, k + 2)
                    for k in range(PAIRS - 3, PAIRS):
                        pair_activations(r, 0, k)
                        if k + 2 < PAIRS:
                            pair_weights(r, 0, k + 2)
                for r in range(GROUPS):
                    dve.wait_ge(o.got[r], 16 * TOP_K * GT)
                    for k in range(TOP_K):
                        dve.drain()
                        for t in range(GT):
                            rows = xs[:, r * GT + t, :]
                            nc.vector.scalar_tensor_tensor(rows, got[r][:, k, t, :], gates[r][:, k, t:t + 1],
                                                           rows, ALU.mult, ALU.add)
                    dve.drain()

            def normed(b):
                dve.wait_ge(s_rr, b + 1)
                for t in range(BT):
                    nc.vector.tensor_scalar(xn[:, t, :], xs[:, bass.ds(b * BT + t, 1), :],
                                            mv[:, t, 0:1], rstd[:, t:t + 1], ALU.subtract, ALU.mult)
                dve.drain().then_inc(s_xn, 1)

            def reduce_bank(u, parity, n):
                pieces, half = BANKS[n]
                h0, it, _, w = pieces[0]
                dst = (nmax1[:, h0:h0 + len(pieces), it - 4] if half
                       else nmax[parity][:, h0:h0 + len(pieces), it])
                dve.wait_ge(s_b1, u * NB + n + 1)
                nc.vector.tensor_reduce(
                    dst, ps_1[n % 2][:, 0:len(pieces) * w].rearrange("p (h j) -> p h j", j=w),
                    axis=AXX, op=ALU.max, negate=True).then_inc(s_red, 1)

            def join_maxima(parity):
                m = nmax[parity]
                dve.drain()
                nc.vector.tensor_tensor(m[:, :, 4:8], m[:, :, 4:8], nmax1[:, :, :], ALU.min)
                dve.drain().then_inc(s_max, 1)

            def use(b, base, i, g, name, u_next):
                if name[:-1] not in ("o", "proj") and name != "max":
                    return
                dve.wait_ge(s_use, base + i + 1)
                if name == "max":
                    if u_next is not None:
                        dve.wait_ge(s_mw, 16 * u_next)
                    m = ps_m[0:GH * BT, 0:P]
                    nc.vector.tensor_copy(mp[:, 0, :], m)
                    dve.drain()
                    nc.vector.tensor_tensor(mrest[:, :], m, mp[:, 0, :], ALU.subtract).then_inc(s_free, 1)
                    dve.drain()
                    nc.vector.tensor_copy(mp[:, 1, :], mrest[:, :])
                    dve.drain()
                    nc.vector.tensor_tensor(mp[:, 2, :], mrest[:, :], mp[:, 1, :], ALU.subtract
                                            ).then_inc(s_mp, 1)
                elif name[0] == "o":
                    ih = int(name[1])
                    gg = g if ih == 0 else (g - 1) % UNITS
                    v = ps_m.rearrange("p (t h c) -> p t h c", t=4, h=GH)
                    nc.vector.reciprocal(rden[:, :, :], v[:, :, :, DH])
                    dve.drain()
                    nc.vector.tensor_tensor(
                        att[:, 4 * ih:4 * ih + 4, gg * GH * DH:(gg + 1) * GH * DH
                            ].rearrange("p t (h d) -> p t h d", d=DH),
                        v[:, :, :, 0:DH], rden[:, :, :].unsqueeze(3).to_broadcast([P, 4, GH, DH]),
                        ALU.mult).then_inc(s_free, 1)
                else:
                    rows = xs[:, bass.ds(b * BT + 4 * int(name[-1]), 4), :]
                    nc.vector.tensor_tensor(rows, ps_m.rearrange("p (t d) -> p t d", t=4), rows,
                                            ALU.add).then_inc(s_free, 1)

            def steps(b0, span, uses, last=False):
                base = len(START) + b0 * len(USES)
                for db, g, s in span:
                    b = b0 + db
                    u = b * UNITS + g
                    banks_now, ahead = banks_at(s)
                    if not (last and g + ahead >= UNITS):
                        for n in banks_now:
                            reduce_bank(u + ahead, (g + ahead) % 2, n)
                        if s == AHEAD - 1:
                            join_maxima((g + 1) % 2)
                    for i, name in numbered(uses, g, s, db):
                        use(b0, base, i, g, name, u + 1)
                    if g == 1 and s == 0 and not last:
                        statistics((b + 1) * BT, BT, 0)
                        dve.drain().then_inc(s_mv, 1)
                    if g == 1 and s == 2 and not last:
                        normed(b + 1)

            if phases[0]:
                run_ffn(0)
            if phases[1]:
                nc.vector.memset(ps_o, 0.0).then_inc(s_oz, 1)
                statistics(0, BT, 0)
                dve.drain().then_inc(s_mv, 1)
                normed(0)
                for n in range(NB):
                    reduce_bank(0, 0, n)
                join_maxima(0)
                use(0, 0, len(START) - 1, 0, "max", None)
                for n in range(EARLY):
                    reduce_bank(1, 1, n)
                steps(0, FIRST_STEPS, [])
                with dve.Fori(0, BATCH - 1) as b:
                    steps(b, BODY_STEPS, USES)
                steps(BATCH - 1, LAST_STEPS, USES_LAST, True)
                for i, (_, _, _, name) in enumerate(END):
                    use(BATCH - 1, len(START) + (BATCH - 1) * len(USES) + len(USES_LAST), i, 0, name, None)
            if phases[2]:
                dve.drain()
                run_ffn(1)
            dve.drain().then_inc(s_done, 1)

        @block.tensor
        def _(pe):
            mm = nc.tensor.matmul
            pe.wait_ge(s_c, 1)
            pe.wait_ge(s_w, 16 * 9)
            nc.tensor.transpose(ps_t[:, 0:EXPERTS], rms_rows[:, :], ident[0:EXPERTS, 0:EXPERTS]
                                ).then_inc(s_rmsT, 1)
            pe.wait_ge(s_wready, 1)

            def run_ffn(f):
                o = ffn[f]

                def transposes(c):
                    pe.wait_ge(o.xh, c + 1)
                    if c:
                        pe.wait_ge(o.xts, c)
                    for t in range(CT):
                        last = nc.tensor.transpose(ps_t[:, t * P:(t + 1) * P], xh[:, c * CT + t, :], ident[:, :])
                    last.then_inc(o.xt, 1)

                def logits(c):
                    pe.wait_ge(o.xts, c + 1)
                    if c >= GC:
                        pe.wait_ge(o.lgs, c // GC)
                    for t in range(CT):
                        at = (c % GC * CT + t) * RS
                        last = mm(ps_l[:, at:at + E_ROUTED], xT[c % 2][:, t * P:(t + 1) * P],
                                  wr[:, :], start=True, stop=True)
                    last.then_inc(o.lg, 1)

                def hidden(n):
                    c, (e, half) = n // NH, HALVES[n % NH]
                    pe.wait_ge(o.u, n + 1)
                    mm(ps_h[n % RING], w1s[:, e, half * P:(half + 1) * P], xT[c % 2][:, :],
                       start=True, stop=True).then_inc(o.h, 1)

                def product(n):
                    c, (e, half) = n // NH, HALVES[n % NH]
                    if n % NH == 0 and c:
                        pe.wait_ge(o.acc, c)
                    pe.wait_ge(o.u, RING + n + 1)
                    for t in range(CT):
                        last = mm(ps_y[0][:, t * D:(t + 1) * D],
                                  uu[n % RING][:, t * P:(t + 1) * P], w2s[:, e, half, :],
                                  start=(n % NH == 0 and t == 0), stop=(n % NH == NH - 1),
                                  skip_group_check=True)
                    last.then_inc(o.used, 1)

                def ranks(r):
                    pe.wait_ge(o.cho, r + 1)
                    if r:
                        pe.wait_ge(o.pos, r)
                    c = chosen[:, :, :].rearrange("p e t -> p (e t)")
                    w = E_ROUTED * GT
                    mm(ps_r[:, 0:w], tri[:, :], c, start=True, stop=True)
                    mm(ps_r[:, 256:256 + w], onesb[:, :], c, start=True, stop=True).then_inc(o.cnt, 1)

                transposes(0)
                logits(0)
                hidden(0)
                hidden(1)
                for n in range(SHARED):
                    c, k = n // NH, n % NH
                    if k == 0 and c + 1 < CHUNKS:
                        transposes(c + 1)
                    if k == 1 and c + 1 < CHUNKS:
                        logits(c + 1)
                    if n + 2 < SHARED:
                        hidden(n + 2)
                    product(n)
                    if (c, k) == (GC - 1, NH - 1):
                        ranks(0)
                ranks(1)

                def pair_transposes(r, i, k):
                    q0 = r * PAIRS + k
                    pe.wait_ge(o.xl[q0 % 2], 16 * (i + q0 // 2 + 1))
                    if not (isinstance(i, int) and q0 + 2 * i < 2):
                        pe.wait_ge(o.pe, 2 * i + q0 - 1)
                    for t in range(2):
                        last = nc.tensor.transpose(ps_tp[q0 % 2][:, t * P:(t + 1) * P], xld[q0 % 2][:, t, :],
                                                   ident[:, :])
                    last.then_inc(o.pt, 1)

                def pair_hidden(r, i, k):
                    q0 = r * PAIRS + k
                    pe.wait_ge(o.pe, 2 * i + q0 + 1)
                    pe.wait_ge(o.w1, 2 * i + q0 + 1)
                    pe.wait_ge(o.u, RING + SHARED + 2 * i + q0 - 1)
                    for half in range(2):
                        for a in range(2):
                            at = (2 * half + a) * P
                            last = mm(ps_h[q0 % 2][:, at:at + P], w1c[q0 % 2][:, a, half * P:(half + 1) * P],
                                      xTp[q0 % 2][:, a * P:(a + 1) * P], start=True, stop=True)
                    last.then_inc(o.h, 1)

                def pair_products(r, i, k):
                    q0 = r * PAIRS + k
                    es = [pe.value_load(tile_e[r][0:1, bass.ds(2 * (2 * i + k) + a, 1)],
                                        min_val=0, max_val=E_ROUTED - 1) for a in range(2)]
                    pe.wait_ge(o.ye, 2 * i + q0 + 1)
                    pe.wait_ge(o.u, RING + SHARED + 2 * i + q0 + 1)
                    for a in range(2):
                        for half in range(2):
                            at = (2 * half + a) * P
                            last = mm(ps_y[q0 % 2][:, a * D:(a + 1) * D], uu[q0 % 2][:, at:at + P],
                                      w2s[:, bass.ds(es[a], 1), half, :], start=(half == 0), stop=(half == 1))
                    last.then_inc(o.used, 1)

                pe.wait_ge(o.pos, GROUPS)
                pe.wait_ge(o.acc, CHUNKS)
                for r in range(GROUPS):
                    pair_transposes(r, 0, 0)
                    pair_transposes(r, 0, 1)
                    pair_hidden(r, 0, 0)
                    with pe.Fori(0, (PAIRS - 3) // 2) as i:
                        for k in range(2):
                            pair_transposes(r, i, k + 2)
                            pair_hidden(r, i, k + 1)
                            pair_products(r, i, k)
                    for k in range(PAIRS - 3, PAIRS):
                        if k + 2 < PAIRS:
                            pair_transposes(r, 0, k + 2)
                        if k + 1 < PAIRS:
                            pair_hidden(r, 0, k + 1)
                        pair_products(r, 0, k)

            def first_pass(u, b, g, n):
                pieces, half = BANKS[n]
                if n == 0:
                    pe.wait_ge(s_rows[g], 16 * 18 * (b + 1))
                pe.wait_ge(s_red, u * NB + n + 1)
                for j, (h, it, j0, w) in enumerate(pieces):
                    dst = ps_1[n % 2][:, j * w:(j + 1) * w]
                    diagonal = j0 + w == (it + 1) * P
                    last = mm(dst, qs[g][0:PASS1_ROWS, h, it * P:(it + 1) * P],
                              ks[g][0:PASS1_ROWS, h, j0:j0 + w], start=True, stop=not diagonal)
                    if diagonal:
                        last = mm(dst[:, w - P:w], identb[:, :], maskb[:, :], start=False, stop=True)
                last.then_inc(s_b1, 1)

            def scores(u, g, s, pair):
                jt, i0, w, ih = STEPS[s]
                pe.wait_ge(s_e, u * 2 * NS + 2 * s + pair + 1)
                for j in range(2):
                    h = 2 * pair + j
                    diagonal = i0 == jt * P
                    last = mm(ps_s[pair][:, j, 0:w], ks[g][:, h, jt * P:(jt + 1) * P],
                              qs[g][:, h, i0:i0 + w], start=True, stop=not diagonal)
                    if diagonal:
                        last = mm(ps_s[pair][:, j, 0:P], maskb[:, :], identb[:, :], start=False, stop=True)
                last.then_inc(s_s, 1)

            def weigh(u, b, g, s):
                jt, i0, w, ih = STEPS[s]
                if jt == 0:
                    pe.wait_ge(s_ot, 2 * u + ih + 1)
                if g == 0 and s <= LAST_OF_HALF[0] or g == 0 and jt > LAST_OF_HALF[0]:
                    pe.wait_ge(s_va, BT * b + jt + 1)
                pe.wait_ge(s_e, 2 + u * 2 * NS + 2 * s + 2)
                for h in range(GH):
                    last = mm(ps_o[32 * h:32 * h + VW, i0 - HALF * ih:HALF],
                              vaug[:, jt, g * GH + h, :], pT[s % 2][h // 2][:, h % 2, 0:w],
                              start=(jt == 0), stop=(s == LAST_OF_HALF[ih]))
                last.then_inc(s_pv, 1)

            def use(b, base, i, name, u, g):
                kind, j = (name, 0) if name == "max" else (name[:-1], int(name[-1]))
                cols = slice(512 * j, 512 * (j + 1))
                if kind == "xn" and j == 0:
                    pe.wait_ge(s_xn, b + 1)
                if kind == "max":
                    pe.wait_ge(s_max, u + 1)
                if kind == "o":
                    pe.wait_ge(s_ot, 1 + 2 * u + j + 1)
                pe.wait_ge(s_free, base + i + 1)
                if kind in ("xn", "att"):
                    src = xn if kind == "xn" else att
                    for t in range(4):
                        last = nc.tensor.transpose(ps_m[:, t * P:(t + 1) * P], src[:, 4 * j + t, :],
                                                   ident[:, :])
                elif kind in ("q", "k"):
                    at = 0 if kind == "q" else D
                    last = mm(ps_m, wqkv[:, at:at + D], xnT[:, cols], start=True, stop=True)
                elif kind in ("v", "proj"):
                    src, w = (xnT, wqkv[:, 2 * D:]) if kind == "v" else (attT, wproj[:, :])
                    for t in range(4):
                        last = mm(ps_m[:, t * D:(t + 1) * D], src[:, (4 * j + t) * P:(4 * j + t + 1) * P], w,
                                  start=True, stop=True)
                elif kind == "max":
                    last = nc.tensor.transpose(ps_m[0:GH * BT, 0:P],
                                               nmax[g % 2][:, :, :].rearrange("p h t -> p (h t)"), ident[:, :])
                else:
                    for t in range(4):
                        last = nc.tensor.transpose(ps_m[:, t * P:(t + 1) * P], oT[j][:, t * P:(t + 1) * P],
                                                   ident[:, :])
                last.then_inc(s_use, 1)

            def steps(b0, span, uses, last=False):
                base = len(START) + b0 * len(USES)
                for db, g, s in span:
                    b = b0 + db
                    u = b * UNITS + g
                    s1, g1 = (s + 1, g) if s + 1 < NS else (0, (g + 1) % UNITS)
                    u1 = u if s + 1 < NS else u + 1
                    more = not (last and g == UNITS - 1 and s == NS - 1)
                    todo, ahead = banks_at(s)
                    if last and g + ahead >= UNITS:
                        todo = []
                    gb, bb = (g + ahead) % UNITS, b + (g + ahead) // UNITS
                    for n in todo[0:1]:
                        first_pass(u + ahead, bb, gb, n)
                    if more and s1 == 0:
                        pe.wait_ge(s_mrow, 16 * (u1 + 1))
                    if more:
                        scores(u1, g1, s1, 0)
                    for n in todo[1:2]:
                        first_pass(u + ahead, bb, gb, n)
                    if more:
                        scores(u1, g1, s1, 1)
                    for n in todo[2:3]:
                        first_pass(u + ahead, bb, gb, n)
                    for i, name in numbered(uses, g, s, db):
                        if name == "max":
                            use(0, base, i, name, u + 1, g + 1)
                        elif name in ("o0", "o1"):
                            use(0, base, i, name, u if name == "o0" else u - 1, 0)
                        else:
                            use(b + 1, base, i, name, 0, 0)
                    weigh(u, b, g, s)
                    for n in todo[3:]:
                        first_pass(u + ahead, bb, gb, n)

            if phases[0]:
                run_ffn(0)
            if phases[1]:
                pe.wait_ge(s_oz, 1)
                pe.wait_ge(s_alr, 16 * UNITS)
                pe.wait_ge(s_ones, 1)
                for i, (_, _, _, name) in enumerate(START[:-1]):
                    use(0, 0, i, name, 0, 0)
                for n in range(NB):
                    first_pass(0, 0, 0, n)
                use(0, 0, len(START) - 1, "max", 0, 0)
                for n in range(EARLY):
                    first_pass(1, 0, 1, n)
                pe.wait_ge(s_mrow, 16)
                scores(0, 0, 0, 0)
                scores(0, 0, 0, 1)
                steps(0, FIRST_STEPS, [])
                with pe.Fori(0, BATCH - 1) as b:
                    steps(b, BODY_STEPS, USES)
                steps(BATCH - 1, LAST_STEPS, USES_LAST, True)
                for i, (_, _, _, name) in enumerate(END):
                    use(0, len(START) + (BATCH - 1) * len(USES) + len(USES_LAST), i, name,
                        BATCH * UNITS - 1, 0)
            if phases[2]:
                run_ffn(1)


def kernel(L0_attn_x, L0_attn_w_qkv, L0_attn_w_proj, L0_ffn_router_w, L0_ffn_rms_w, L0_ffn_w1,
           L0_ffn_w2, L0_ffn_rms_w_s, L0_ffn_w1_s, L0_ffn_w2_s):
    import numpy as np
    import concourse.bacc as bacc
    from concourse.bass_utils import run_bass_kernel_spmd

    start = 2.0 ** (-2.0 ** (-(math.log2(HEADS) - 3)))
    slopes = np.array([start * start ** i for i in range(HEADS)], np.float32)
    alibi = slopes[:, None] * np.arange(SEQ, dtype=np.float32)[None, :]

    nc = bacc.Bacc("TRN2", target_bir_lowering=False, num_devices=1)
    arrays, aps = {}, []
    for name, a in (("x", L0_attn_x), ("w_qkv", L0_attn_w_qkv), ("w_proj", L0_attn_w_proj),
                    ("router_w", L0_ffn_router_w), ("rms_w", L0_ffn_rms_w), ("w1", L0_ffn_w1),
                    ("w2", L0_ffn_w2), ("rms_w_s", L0_ffn_rms_w_s), ("w1_s", L0_ffn_w1_s),
                    ("w2_s", L0_ffn_w2_s), ("alibi", alibi)):
        a = np.ascontiguousarray(a)
        arrays[name] = a
        aps.append(nc.dram_tensor(name, a.shape, mybir.dt.from_np(a.dtype), kind="ExternalInput").ap())
    out = nc.dram_tensor("out", (BATCH, SEQ, D), F32, kind="ExternalOutput").ap()

    def by_tile(a):
        return a.rearrange("b (t p) d -> p (b t) d", p=P)

    build(nc, by_tile(aps[0]), *aps[1:], by_tile(out))
    r = run_bass_kernel_spmd(nc, [arrays], core_ids=[0])
    return r.results[0]["out"]
```

```python
import math
from contextlib import ExitStack

import concourse.bass as bass
import numpy as np
from concourse import mybir
from concourse.alu_op_type import AluOpType as ALU

F32 = mybir.dt.float32
BF16 = mybir.dt.bfloat16
U32 = mybir.dt.uint32
I32 = mybir.dt.int32
ACT = mybir.ActivationFunctionType
AXX = mybir.AxisListType.X

P = 128
BATCH, SEQ, D = 4, 1024, 128
HEADS, DH = 16, 8
HID = 256
E_ROUTED, E_SHARED = 14, 2
EXPERTS = E_ROUTED + E_SHARED
LN_EPS, RMS_EPS, GATE_EPS = 1e-5, 1.1920929e-07, 1e-9

TILES = BATCH * SEQ // P
BT = SEQ // P
CT = 4
CHUNK = CT * P
CHUNKS = TILES // CT

HALVES = [(e, half) for e in range(E_ROUTED, EXPERTS) for half in range(2)]
NH = len(HALVES)
SHARED = NH * CHUNKS // 2
RING = 4

GROUPS = 2
GT = TILES // GROUPS
GC = CHUNKS // GROUPS
TOP_K = 2
RTILES = (TOP_K * GT * P + E_ROUTED * (P - 1)) // P
PAIRS = (RTILES + 1) // 2
RTILES = 2 * PAIRS
RS = 16
UNROLL = 4
LOOPS = (5, 2)
ROUTED = GROUPS * PAIRS
LATE = SHARED + ROUTED
BLOCK = 4
BLOCKS = GT // BLOCK

GH = 4
UNITS = HEADS // GH
PARTS = 3
TERMS = PARTS * PARTS * DH
PASS1_ROWS = TERMS + PARTS
PASS2_ROWS = PASS1_ROWS + PARTS
HALF = 512
VW = DH + 1
MASKED = -1e30

STEPS = [(jt, max(HALF * ih, P * jt), HALF * (ih + 1) - max(HALF * ih, P * jt), ih)
         for ih in range(2) for jt in range(4 * (ih + 1))]
NS = len(STEPS)
LAST_OF_HALF = {0: 3, 1: NS - 1}


def first_pass_banks():
    banks = []
    for it in range(BT):
        if it >= 4:
            banks += [([(h, it, 0, HALF)], 0) for h in range(GH)]
        width = P * (it % 4 + 1)
        each = {1: 4, 2: 2, 3: 1, 4: 1}[it % 4 + 1]
        for h0 in range(0, GH, each):
            banks.append(([(h, it, HALF * (it // 4), width) for h in range(h0, h0 + each)], it // 4))
    return banks


BANKS = first_pass_banks()
NB = len(BANKS)
BANKS_IN = [3, 3, 3, 3, 4, 4, 3, 3, 2, 3, 4, 3]
AHEAD = 8
EARLY = sum(BANKS_IN[AHEAD:])
assert sum(BANKS_IN) == NB


def banks_at(s):
    if s < AHEAD:
        first = EARLY + sum(BANKS_IN[:s])
        return range(first, first + BANKS_IN[s]), 1
    first = sum(BANKS_IN[AHEAD:s])
    return range(first, first + BANKS_IN[s]), 2


TURN = 6
FIRST_STEPS = [(0, 0, s) for s in range(TURN)]
BODY_STEPS = ([(0, 0, s) for s in range(TURN, NS)] + [(0, g, s) for g in range(1, UNITS) for s in range(NS)]
              + [(1, 0, s) for s in range(TURN)])
LAST_STEPS = BODY_STEPS[:-TURN]


def uses_at(g, s):
    at = []
    if s == 1:
        at.append("o1")
    if s == 7:
        at.append("o0")
    if s == 8:
        at.append("max")
    if g == 0 and 2 <= s <= 5:
        at.append(("att0", "att1", "proj0", "proj1")[s - 2])
    if g == 1 and s in (3, 4, 5, 6, 9, 10, 11):
        at.append({3: "xn0", 4: "xn1", 5: "q0", 6: "q1", 9: "k0", 10: "k1", 11: "v0"}[s])
    if g == 2 and s == 0:
        at.append("v1")
    return at


NEXT_BATCHS = ("xn0", "xn1", "q0", "q1", "k0", "k1", "v0", "v1")
START = [(0, 0, 0, n) for n in (*NEXT_BATCHS, "max")]
USES = [(db, g, s, n) for db, g, s in BODY_STEPS for n in uses_at(g, s)]
USES_LAST = [(db, g, s, n) for db, g, s in LAST_STEPS for n in uses_at(g, s)
             if n not in NEXT_BATCHS and (g, s, n) != (UNITS - 1, 8, "max")]
END = [(1, 0, 1, "o1"), (1, 0, 2, "att0"), (1, 0, 3, "att1"), (1, 0, 4, "proj0"), (1, 0, 5, "proj1")]


def numbered(uses, g, s, db=0):
    return [(i, n) for i, (d, ug, us, n) in enumerate(uses) if (d, ug, us) == (db, g, s)]


CHOOSE_AT = [1, 2, 3, 4, 5]
PLACE_AT = [8, 9, 10, 11, 12]
EXPS_AT = 4
RANKS_CHUNK = [4, 4]
RANKS_AT = 6
ADD_AT = [8, 9, 12, 13, 15, 16, 18, 19]
STATS_PAIRS = [17, 18]
NORMED_AT = 20
PROLOGUE_PAIRS = [21, 22]
STEPS_ADD_AT = [0, 0, 1, 1, 2, 3, 4, 5]
PROLOGUE_LATE = len(NEXT_BATCHS) - len(PROLOGUE_PAIRS)
LATE_ADD_AT = [8, 9, 12, 13, 15]
Q_PARTS_FROM, K_PARTS_FROM = 1, 5


POOLS_BATCH = 2
POOLS_CHUNKS = range(POOLS_BATCH * BT // CT, (POOLS_BATCH + 1) * BT // CT)
STATS_AT = [7, 8, 9, 10]
NORM_TILES = BT // len(STATS_AT)
NORMED_IN = [3, 3, 2]


def build(nc, x, x_rows, w_qkv, w_proj, router_w, rms_w, w1, w2, rms_w_s, w1_s, w2_s, alibi, out):
    ctx = ExitStack()
    with ctx:
        def sb(name, shape, dt=F32):
            return ctx.enter_context(nc.sbuf_tensor(name, shape, dt))

        def sem(name):
            return ctx.enter_context(nc.semaphore(name))

        xs = sb("xs", [P, TILES, D])
        w12 = sb("w12", [P, EXPERTS, 2 * HID])
        w1s = w12[:, :, 0:HID]
        w2s = w12[:, :, HID:2 * HID].rearrange("p e (c d) -> p e c d", d=D)
        wr = sb("wr", [P, E_ROUTED])
        rms_rows = sb("rms_rows", [EXPERTS, D])
        rms_cols = sb("rms_cols", [P, EXPERTS])
        wqkv = sb("wqkv", [P, 3 * D])
        wproj = sb("wproj", [P, D])
        ident = sb("ident", [P, P])
        identb = sb("identb", [P, P], BF16)
        maskb = sb("maskb", [P, P], BF16)
        experts_row = sb("experts_row", [P, E_ROUTED])
        minus_half = sb("minus_half", [P, GT])
        ln_eps = sb("ln_eps", [P, GT])
        one = sb("one", [P, 1])
        stats = sb("stats", [P, GT, 6])
        mv = sb("mv", [P, TILES, 2])
        var_eps = sb("var_eps", [P, GT])
        rstd = sb("rstd", [P, GT])
        ms = sb("ms", [P, GT])
        rr = sb("rr", [P, TILES])
        inv_rms = sb("inv_rms", [P, TILES])
        xT2 = [sb(f"xT{i}", [P, CHUNK]) for i in range(2)]
        work = sb("work", [P, 2 * RING, CHUNK])
        th = [work[:, i, :] for i in range(RING)]
        uu = [work[:, RING + i, :] for i in range(RING)]
        mx8 = sb("mx8", [P, GT, 8])
        ix8 = sb("ix8", [P, GT, 8], U32)
        ixf = sb("ixf", [P, GT, TOP_K])
        chosen = sb("chosen", [P, E_ROUTED, GT], BF16)
        posf = sb("posf", [P, TOP_K, GT])
        pos = [sb(f"pos{i}", [P, TOP_K, GT], U32) for i in range(GROUPS)]
        ntiles = sb("ntiles", [P, E_ROUTED])
        ends = sb("ends", [P, E_ROUTED])
        base_row = sb("base_row", [P, E_ROUTED])
        tile_ef = sb("tile_ef", [1, RTILES])
        pair_e = [sb(f"pair_e{i}", [1, PAIRS], I32) for i in range(GROUPS)]
        esum = sb("esum", [P, GT])
        gates = [sb(f"gates{i}", [P, TOP_K, GT]) for i in range(GROUPS)]
        xld = [sb(f"xld{i}", [P, 2, D]) for i in range(2)]
        xTp = [sb(f"xTp{i}", [P, 2 * P]) for i in range(2)]
        ysb = [sb(f"ysb{i}", [P, 2, D]) for i in range(2)]
        tri = sb("tri", [P, P], BF16)
        onesb = sb("onesb", [P, P], BF16)
        go_on = sb("go_on", [P, E_ROUTED, GT])
        ones_e = sb("ones_e", [P, E_ROUTED])
        hundreds = sb("hundreds", [P, GT])
        tiles_row = sb("tiles_row", [1, RTILES])
        region_a = sb("region_a", [P, 4, SEQ])
        region_b = sb("region_b", [P, 4, SEQ])
        region_c = sb("region_c", [P, 4, SEQ])
        taken = [0]

        def table(*dims, rows=P):
            at = taken[0]
            taken[0] += int(np.prod(dims))
            assert taken[0] <= 4 * SEQ
            flat = region_a[0:rows, :, :].rearrange("p a n -> p (a n)")[:, at:taken[0]]
            if len(dims) == 2:
                return flat.rearrange("p (a b) -> p a b", b=dims[1])
            return flat.rearrange("p (a b c) -> p a b c", b=dims[1], c=dims[2])

        lg = table(GT, E_ROUTED)
        below = table(GT, E_ROUTED + 1)
        ex = table(GT, E_ROUTED + 1)
        hot = table(TOP_K, GT, E_ROUTED)
        seen = table(E_ROUTED, GT)
        rank = table(E_ROUTED, GT)
        picked = table(TOP_K, GT, E_ROUTED)
        more_than = table(E_ROUTED, GT)
        ended = table(RTILES, E_ROUTED, rows=1)
        xn = region_a[:, 0, :].rearrange("p (t d) -> p t d", d=D)
        xnT = region_a[:, 1, :]
        qf = region_a[:, 2, :]
        kf = region_a[:, 3, :]
        att = region_b[:, 0, :].rearrange("p (t d) -> p t d", d=D)
        attT = region_b[:, 1, :]
        rest = region_b[:, 2, :]
        vst = region_b[:, 3, :].rearrange("p (t d) -> p t d", d=D)
        xh = region_b.rearrange("p a (t d) -> p (a t) d", d=D)

        def xh_tile(t):
            return xh[:, (t + GT) % TILES, :]

        got = [region.rearrange("p a (k t d) -> p (a k t) d", d=D, k=2).rearrange(
            "p (k t) d -> p k t d", k=TOP_K) for region in (region_a, region_c)]
        more_xT = region_a.rearrange("p a n -> p (a n)")[:, taken[0]:taken[0] + 2 * CHUNK]
        assert taken[0] + 2 * CHUNK <= 4 * SEQ
        xT = [xT2[0][:, :], xT2[1][:, :], more_xT[:, 0:CHUNK], more_xT[:, CHUNK:2 * CHUNK]] + th
        w12c = [region_c[:, i, :].rearrange("p (a f) -> p a f", a=2) for i in range(UNROLL)]
        qp = sb("qp", [P, PARTS, SEQ], BF16)
        kp_f = sb("kp", [P, PARTS * SEQ // 2])
        kp = kp_f[:, :].bitcast(BF16).rearrange("p (c n) -> p c n", n=SEQ)
        vaug = sb("vaug", [P, BT, HEADS, VW])
        late_rows = region_c[:, :, :].rearrange("p a n -> p (a n)").bitcast(BF16).rearrange(
            "p (a h n) -> p a h n", a=2, h=GH)[0:PASS2_ROWS]
        qs = [sb(f"qs{g}", [PASS2_ROWS, GH, SEQ], BF16) for g in range(UNITS - 1)] + [late_rows[:, 0]]
        ks = [sb(f"ks{g}", [PASS2_ROWS, GH, SEQ], BF16) for g in range(UNITS - 1)] + [late_rows[:, 1]]
        ONES_FROM = 64
        pT = [[work[:, 4 * i + 2 * j:4 * i + 2 * j + 2, :] for j in range(2)] for i in range(2)]
        nmax = [sb(f"nmax{i}", [P, GH, BT]) for i in range(2)]
        nmax1 = sb("nmax_late_keys", [P, GH, 4])
        mrest = sb("mrest", [GH * BT, P])
        mp = sb("mp", [GH * BT, PARTS, P], BF16)
        oT = [sb(f"oT{i}", [P, HALF]) for i in range(2)]
        rden = sb("rden", [P, 4, GH])
        al = kp_f[:, 0:SEQ]
        al_rest = vaug[:, :, :, :].rearrange("p t h c -> p (t h c)")[:, 0:SEQ]
        ap = qp

        sorted_x = [nc.dram_tensor(f"sorted_x{i}", [RTILES * P, D], F32, kind="Internal").ap()
                    for i in range(GROUPS)]
        sorted_y = [nc.dram_tensor(f"sorted_y{i}", [RTILES * P, D], F32, kind="Internal").ap()
                    for i in range(GROUPS)]
        q_scr = nc.dram_tensor("q_scr", [5, DH, HEADS, SEQ], BF16, kind="Internal").ap()
        k_scr = nc.dram_tensor("k_scr", [PARTS, DH, HEADS, SEQ], BF16, kind="Internal").ap()
        a_scr = nc.dram_tensor("a_scr", [PARTS, HEADS, SEQ], BF16, kind="Internal").ap()
        m_scr = nc.dram_tensor("m_scr", [2, PARTS, GH, BT, P], BF16, kind="Internal").ap()

        banks = ctx.enter_context(nc.psum_tensor("banks", [P, 8, 512], F32))
        ps_h = [banks[:, i, :] for i in range(RING)]
        ps_y = [banks[:, 4 + i, :] for i in range(2)]
        ps_l = banks[:, 5, :]
        ps_t = [banks[:, 6, :], banks[:, 4, :]]
        ps_r = banks[:, 7, :]
        ps_tp = [banks[:, 2 + i, :] for i in range(2)]
        ps_s = [banks[:, 2 * i:2 * i + 2, :] for i in range(2)]
        ps_1 = [banks[:, 4 + i, :] for i in range(2)]
        ps_o = banks[:, 6, :]
        ps_m = banks[:, 7, :]

        s_x = [sem(f"x_loaded{i}") for i in range(BATCH)]
        s_fill = [sem(f"sorted_filled{i}") for i in range(GROUPS)]
        s_wsh = sem("shared_weights_loaded")
        s_wrt = sem("routed_weights_loaded")
        s_wat = sem("attention_weights_loaded")
        s_al = sem("bias_loaded")
        s_id = sem("identity_made")
        s_c = sem("constants_made")
        s_rmsT = sem("rms_transposed")
        s_wready = sem("weights_ready")
        class Ffn:
            pass
        ffn = []
        for f in range(2):
            o = Ffn()
            o.mv = sem(f"f{f}_stats")
            o.rr = sem(f"f{f}_rstd")
            o.xh = sem(f"f{f}_normed")
            o.xh2 = sem(f"f{f}_third_batch_normed")
            o.xt = sem(f"f{f}_transposed")
            o.xts = sem(f"f{f}_transposed_in_sbuf")
            o.lg = sem(f"f{f}_logits")
            o.lgs = sem(f"f{f}_logits_below_max")
            o.ex = sem(f"f{f}_exps")
            o.h = sem(f"f{f}_hidden")
            o.t = sem(f"f{f}_tanh")
            o.u = sem(f"f{f}_act_ready")
            o.used = sem(f"f{f}_act_used")
            o.acc = sem(f"f{f}_shared_added")
            o.cho = sem(f"f{f}_experts_chosen")
            o.cnt = sem(f"f{f}_ranks")
            o.pos = sem(f"f{f}_rows_known")
            o.sc = [sem(f"f{f}_scattered{i}") for i in range(GROUPS)]
            o.xl = [sem(f"f{f}_rows_in{i}") for i in range(2)]
            o.pt = sem(f"f{f}_pair_transposed")
            o.pe = sem(f"f{f}_pair_in_sbuf")
            o.w1 = sem(f"f{f}_pair_weights")
            o.ye = sem(f"f{f}_pair_out_in_sbuf")
            o.ys = [sem(f"f{f}_rows_out{i}") for i in range(2)]
            o.got = [[sem(f"f{f}_gathered{i}_{j}") for j in range(BLOCKS)] for i in range(GROUPS)]
            o.add = sem(f"f{f}_block_added")
            ffn.append(o)
        s_mv = sem("a_stats")
        s_rr = sem("a_rstd")
        s_xn = sem("a_normed")
        s_use = sem("a_shared_bank_filled")
        s_free = sem("a_shared_bank_read")
        s_parts = sem("a_parts_made")
        s_alp = sem("a_bias_parts_made")
        s_ones = sem("a_ones_set")
        s_alw = sem("a_bias_written")
        s_alr = sem("a_bias_rows")
        s_pw = sem("a_parts_written")
        s_rows = [sem(f"a_rows_loaded{g}") for g in range(UNITS)]
        s_mp = sem("a_max_parts")
        s_mw = sem("a_max_written")
        s_mrow = sem("a_max_rows")
        s_va = sem("a_values_ready")
        s_b1 = sem("a_first_pass_bank")
        s_red = sem("a_first_pass_reduced")
        s_s = sem("a_scores")
        s_e = sem("a_probs")
        s_pv = sem("a_outputs")
        s_ot = sem("a_output_in_sbuf")
        s_max = sem("a_maxima")
        s_oz = sem("a_output_bank_zeroed")
        s_out = sem("result_written")

        block = ctx.enter_context(nc.Block())

        @block.sync
        def _(sp):
            def load_batch(b):
                sp.dma_start(xs[:, b * BT:(b + 1) * BT, :], x[:, b * BT:(b + 1) * BT, :]).then_inc(s_x[b], 16)

            for b in range(GT // BT):
                load_batch(b)
            for dst, src in ((wr[:, :], router_w),
                             (rms_rows[0:E_ROUTED, :], rms_w), (rms_rows[E_ROUTED:EXPERTS, :], rms_w_s),
                             (w1s[:, E_ROUTED:EXPERTS, :], w1_s.rearrange("e d f -> d e f")),
                             *[(w2s[:, E_ROUTED:EXPERTS, c, :], w2_s[:, c * P:(c + 1) * P, :].rearrange(
                                 "e p d -> p e d")) for c in range(2)]):
                sp.dma_start(dst, src).then_inc(s_wsh, 16)
            for b in range(GT // BT, BATCH):
                load_batch(b)

            def fill(i):
                for at in range(0, RTILES, TILES):
                    n = min(TILES, RTILES - at)
                    sp.dma_start(sorted_x[i][at * P:(at + n) * P, :], x_rows[0:n * P, :]).then_inc(s_fill[i], 16)

            fill(0)
            for dst, src in ((w1s[:, 0:E_ROUTED, :], w1.rearrange("e d f -> d e f")),
                             *[(w2s[:, 0:E_ROUTED, c, :], w2[:, c * P:(c + 1) * P, :].rearrange(
                                 "e p d -> p e d")) for c in range(2)]):
                sp.dma_start(dst, src).then_inc(s_wrt, 16)
            fill(1)
            for dst, src in ((wqkv[:, :], w_qkv), (wproj[:, :], w_proj)):
                sp.dma_start(dst, src).then_inc(s_wat, 16)
            sp.dma_start(al[0:HEADS, :], alibi).then_inc(s_al, 16)

            def write_bias():
                sp.wait_ge(s_alp, 1)
                sp.dma_start(a_scr.rearrange("c h n -> h c n"), ap[0:HEADS, :, :]).then_inc(s_alw, 16)
                sp.wait_ge(s_alw, 16)
                sp.wait_ge(s_ones, 1)
                for g in range(UNITS - 1):
                    bias_rows(g)

            def bias_rows(g):
                sp.dma_start(ks[g][TERMS:PASS1_ROWS, :, :],
                             a_scr[:, g * GH:(g + 1) * GH, :]).then_inc(s_alr, 16)

            def write_parts(b):
                sp.wait_ge(s_parts, 2 * b + 1)
                for c in range(5):
                    sp.dma_start(q_scr[c].rearrange("d h n -> h d n"), qp[:, c % PARTS, :]).then_inc(s_pw, 16)
                sp.wait_ge(s_parts, 2 * b + 2)
                for c in range(PARTS):
                    sp.dma_start(k_scr[c].rearrange("d h n -> h d n"), kp[:, c, :]).then_inc(s_pw, 16)
                sp.wait_ge(s_pw, 128 * b + 128)

            def load_rows(g):
                for a in range(PARTS):
                    rows = slice(a * PARTS * DH, (a + 1) * PARTS * DH)
                    for dst, src in ((qs[g], q_scr[a:a + PARTS]), (ks[g], k_scr)):
                        sp.dma_start(dst[rows, :, :], src[:, :, g * GH:(g + 1) * GH, :].rearrange(
                            "c d h n -> (c d) h n")).then_inc(s_rows[g], 16)

            def max_rows(b, g):
                u = b * UNITS + g
                sp.wait_ge(s_mp, u + 1)
                sp.dma_start(m_scr[g % 2].rearrange("c h t p -> (h t) c p"), mp[:, :, :]).then_inc(s_mw, 16)
                sp.wait_ge(s_mw, 16 * u + 16)
                sp.dma_start(qs[g][PASS1_ROWS:PASS2_ROWS, :, :],
                             m_scr[g % 2].rearrange("c h t p -> c h (t p)")).then_inc(s_mrow, 16)

            def rows_of(b, g, before):
                sp.wait_ge(s_pv, 2 + (before * UNITS + g + 1) * NS)
                load_rows(g)

            def pairs(f):
                o = ffn[f]

                def load(r, i, k):
                    q0 = r * PAIRS + k
                    if k >= 2 or r:
                        sp.wait_ge(o.pt, UNROLL * i + q0 - 1)
                    rows = sorted_x[r].rearrange("(j t p) d -> j p t d", p=P, t=2)
                    sp.dma_start(xld[q0 % 2][:, :, :], rows[bass.ds(UNROLL * i + k, 1)].rearrange(
                        "j p t d -> (j p) t d")).then_inc(o.xl[q0 % 2], 16)

                for r in range(GROUPS):
                    sp.wait_ge(o.sc[r], 16 * TOP_K * GT)
                    load(r, 0, 0)
                    load(r, 0, 1)
                    with sp.Fori(0, LOOPS[r]) as i:
                        for k in range(UNROLL):
                            load(r, i, k + 2)
                    for k in range(UNROLL * LOOPS[r] + 2, PAIRS):
                        load(r, 0, k)

            pairs(0)
            write_bias()
            write_parts(0)
            for g in range(UNITS - 1):
                load_rows(g)
            max_rows(0, 0)
            sp.wait_ge(ffn[0].add, GROUPS * BLOCKS)
            for rows in (qs[UNITS - 1][TERMS:PASS1_ROWS], ks[UNITS - 1][PASS1_ROWS:PASS2_ROWS]):
                sp.dma_start(rows, ks[0][PASS1_ROWS:PASS2_ROWS, :, :]).then_inc(s_alr, 16)
            bias_rows(UNITS - 1)
            load_rows(UNITS - 1)
            with sp.Fori(0, BATCH - 1) as b:
                max_rows(b, 1)
                max_rows(b, 2)
                write_parts(b + 1)
                rows_of(b + 1, 0, b)
                max_rows(b, 3)
                rows_of(b + 1, 1, b)
                max_rows(b + 1, 0)
                rows_of(b + 1, 2, b)
                rows_of(b + 1, 3, b)
            for g in range(1, UNITS):
                max_rows(BATCH - 1, g)
            pairs(1)
            for t in range(0, TILES, BLOCK):
                sp.wait_ge(ffn[1].add, t // BLOCK + 1)
                sp.dma_start(out[:, t:t + BLOCK, :], xs[:, t:t + BLOCK, :]).then_inc(s_out, 16)
            sp.wait_ge(s_out, 16 * (TILES // BLOCK))

        @block.gpsimd
        def _(pool):
            nc.gpsimd.memset(ident[:, :], 0.0)
            pool.drain()
            nc.gpsimd.affine_select(out=ident[:, :], in_=ident[:, :], compare_op=ALU.not_equal, fill=1.0,
                                    base=0, pattern=[[-1, P]], channel_multiplier=1)
            pool.drain().then_inc(s_id, 1)
            nc.gpsimd.memset(identb[:, :], 0.0)
            nc.gpsimd.memset(maskb[:, :], 0.0)
            nc.gpsimd.memset(minus_half[:, :], -0.5)
            nc.gpsimd.memset(ln_eps[:, :], LN_EPS)
            nc.gpsimd.memset(one[:, :], 1.0)
            nc.gpsimd.memset(tri[:, :], 1.0)
            nc.gpsimd.memset(onesb[:, :], 1.0)
            nc.gpsimd.memset(ones_e[:, :], 1.0)
            nc.gpsimd.memset(go_on[:, :, :], 1.0)
            nc.gpsimd.iota(experts_row[:, :], pattern=[[1, E_ROUTED]], base=0, channel_multiplier=0,
                           allow_small_or_imprecise_dtypes=True)
            nc.gpsimd.iota(hundreds[:, :], pattern=[[P, GT]], base=0, channel_multiplier=0,
                           allow_small_or_imprecise_dtypes=True)
            nc.gpsimd.iota(tiles_row[:, :], pattern=[[1, RTILES]], base=0, channel_multiplier=0,
                           allow_small_or_imprecise_dtypes=True)
            pool.drain()
            nc.gpsimd.affine_select(out=identb[:, :], in_=identb[:, :], compare_op=ALU.not_equal, fill=1.0,
                                    base=0, pattern=[[-1, P]], channel_multiplier=1)
            nc.gpsimd.affine_select(out=tri[:, :], in_=tri[:, :], compare_op=ALU.is_gt, fill=0.0,
                                    base=0, pattern=[[1, P]], channel_multiplier=-1)
            nc.gpsimd.memset(go_on[:, :, 0:1], 0.0)
            nc.gpsimd.affine_select(out=maskb[:, :], in_=maskb[:, :], compare_op=ALU.is_ge, fill=MASKED,
                                    base=0, pattern=[[-1, P]], channel_multiplier=1)
            pool.drain().then_inc(s_c, 1)

            def powers(t0, n, rms):
                v = slice(t0, t0 + n)
                w = slice(0, n)
                nc.gpsimd.tensor_tensor(var_eps[:, w], mv[:, v, 1], ln_eps[:, w], ALU.add)
                pool.drain()
                nc.gpsimd.tensor_tensor(rstd[:, w], var_eps[:, w], minus_half[:, w], ALU.pow)
                pool.drain()
                if not rms:
                    return
                nc.gpsimd.tensor_tensor(ms[:, w], mv[:, v, 1], rstd[:, w], ALU.mult)
                pool.drain()
                nc.gpsimd.tensor_tensor(ms[:, w], ms[:, w], rstd[:, w], ALU.mult)
                pool.drain()
                nc.gpsimd.tensor_scalar(ms[:, w], ms[:, w], RMS_EPS, None, ALU.add)
                pool.drain()
                nc.gpsimd.tensor_tensor(rr[:, v], ms[:, w], minus_half[:, w], ALU.pow)
                pool.drain()
                nc.gpsimd.tensor_tensor(inv_rms[:, v], ms[:, w], rr[:, v], ALU.mult)
                pool.drain()
                nc.gpsimd.tensor_tensor(rr[:, v], rr[:, v], rstd[:, w], ALU.mult)
                pool.drain()

            def ffn_norms(f):
                o = ffn[f]
                for b in range(BATCH):
                    pool.wait_ge(o.mv, b + 1)
                    powers(b * BT, BT, True)
                    if b != POOLS_BATCH:
                        pool.drain().then_inc(o.rr, 1)
                        continue
                    if f:
                        pool.wait_ge(s_free, 1 + len(START) + (BATCH - 1) * len(USES) + len(USES_LAST) + len(END))
                    for c in range(b * BT // CT, (b + 1) * BT // CT):
                        for t in range(c * CT, (c + 1) * CT):
                            nc.gpsimd.tensor_scalar(xh_tile(t), xs[:, t, :], mv[:, t, 0:1], rr[:, t:t + 1],
                                                    ALU.subtract, ALU.mult)
                        pool.drain().then_inc(o.xh2, 1)

            def scatter(f, r):
                o = ffn[f]
                pool.wait_ge(o.pos, r + 1)
                pool.wait_ge(s_fill[r], 16 * -(-RTILES // TILES))
                for t in range(GT):
                    for k in range(TOP_K):
                        nc.gpsimd.indirect_dma_start(
                            out=sorted_x[r], out_offset=bass.IndirectOffsetOnAxis(ap=pos[r][:, k, t:t + 1], axis=0),
                            in_=xh_tile(r * GT + t), in_offset=None).then_inc(o.sc[r], 16)

            def gather(f, r):
                o = ffn[f]
                for i in range(2):
                    pool.wait_ge(o.ys[i], 16 + 16 * sum(q % 2 == i for q in range((r + 1) * PAIRS)))
                for t in range(GT):
                    for k in range(TOP_K):
                        nc.gpsimd.indirect_dma_start(
                            out=got[r][:, k, t, :], out_offset=None, in_=sorted_y[r],
                            in_offset=bass.IndirectOffsetOnAxis(ap=pos[r][:, k, t:t + 1], axis=0),
                            ).then_inc(o.got[r][t // BLOCK], 16)

            def split(src, parts, tmp, n):
                nc.gpsimd.tensor_tensor(parts[:n, 0, :], src[:n, :], one[:n, :].to_broadcast([n, SEQ]), ALU.mult)
                pool.drain()
                nc.gpsimd.tensor_tensor(tmp[:n, :], src[:n, :], parts[:n, 0, :], ALU.subtract)
                pool.drain()
                nc.gpsimd.tensor_copy(parts[:n, 1, :], tmp[:n, :])
                pool.drain()
                nc.gpsimd.tensor_tensor(parts[:n, 2, :], tmp[:n, :], parts[:n, 1, :], ALU.subtract)

            def values(b):
                v = vst[:, :, :].rearrange("p t (h d) -> p t h d", d=DH)
                for jt in range(BT):
                    if not isinstance(b, int):
                        pool.wait_ge(s_pv, 2 + b * UNITS * NS - (BT - 1 - jt))
                    nc.gpsimd.tensor_tensor(vaug[:, jt, :, 0:DH], v[:, jt, :, :],
                                            one[:, :].unsqueeze(2).to_broadcast([P, HEADS, DH]),
                                            ALU.mult).then_inc(s_va, 1)

            def norm(b):
                pool.wait_ge(s_mv, b + 1)
                powers(0, BT, False)
                pool.drain().then_inc(s_rr, 1)

            def make_parts(b, base, names):
                at = {n: i for i, (_, _, _, n) in enumerate(names)}
                pool.wait_ge(s_free, base + at["q1"] + 2)
                pool.wait_ge(s_pw, 128 * b)
                split(qf, qp, rest, P)
                pool.drain().then_inc(s_parts, 1)
                pool.wait_ge(s_free, base + at["k1"] + 2)
                split(kf, kp, rest, P)
                pool.drain().then_inc(s_parts, 1)

            def ones(g):
                pool.drain()
                nc.gpsimd.memset(ks[g][ONES_FROM:PASS2_ROWS, :, :], 1.0)
                nc.gpsimd.memset(qs[g][ONES_FROM:PASS2_ROWS, :, :], 1.0)

            ffn_norms(0)
            scatter(0, 0)
            scatter(0, 1)
            pool.wait_ge(s_al, 16)
            split(al, ap, al_rest, HEADS)
            pool.drain().then_inc(s_alp, 1)
            for g in range(UNITS - 1):
                ones(g)
            pool.drain()
            nc.gpsimd.memset(vaug[:, :, :, DH:VW], 1.0)
            pool.drain().then_inc(s_ones, 1)
            gather(0, 0)
            norm(0)
            pool.wait_ge(s_free, 1 + len(START) - 1)
            values(0)
            gather(0, 1)
            with pool.Fori(0, BATCH - 1) as b:
                norm(b + 1)
                make_parts(b + 1, len(START) + b * len(USES), USES)
                pool.wait_ge(s_free, 2 + len(START) + b * len(USES) + [u[3] for u in USES].index("v1"))
                values(b + 1)
            ffn_norms(1)
            for r in range(GROUPS):
                scatter(1, r)
            for r in range(GROUPS):
                gather(1, r)

        @block.scalar
        def _(act):
            def transposed(f, i):
                o = ffn[f]
                act.wait_ge(o.xt, i + 1)
                if i < CHUNKS:
                    nc.scalar.activation(xT[i], ps_t[i % 2], ACT.Copy).then_inc(o.xts, 1)
                else:
                    act.wait_ge(o.h, LATE + NH * (i - CHUNKS - 1) if i >= CHUNKS + 2 else SHARED)
                    nc.scalar.activation(xT[i % 2], ps_t[0], ACT.Copy).then_inc(o.xts, 1)

            def exps(f, r):
                act.wait_ge(ffn[f].lgs, r + 1)
                nc.scalar.activation(ex[:, :, :], below[:, :, :], ACT.Exp).then_inc(ffn[f].ex, 1)

            def run_ffn(f, prologue=False):
                o = ffn[f]

                def tanh(n):
                    act.wait_ge(o.h, n + 1)
                    nc.scalar.activation(th[n % RING], ps_h[n % RING], ACT.Tanh, scale=0.5).then_inc(o.t, 1)

                for c in range(GC, CHUNKS):
                    if c == RANKS_CHUNK[f]:
                        exps(f, 0)
                    transposed(f, c)
                for n in range(SHARED):
                    tanh(n)
                    if n == EXPS_AT:
                        exps(f, 1)

                def bring(r, i, k):
                    q0 = r * PAIRS + k
                    act.wait_ge(o.pt, UNROLL * i + q0 + 1)
                    act.wait_ge(o.h, SHARED + UNROLL * i + q0 - 1)
                    nc.scalar.activation(xTp[q0 % 2][:, :], ps_tp[q0 % 2][:, 0:2 * P],
                                         ACT.Copy).then_inc(o.pe, 1)

                def pair_tanh(r, i, k):
                    q0 = r * PAIRS + k
                    act.wait_ge(o.h, SHARED + UNROLL * i + q0 + 1)
                    nc.scalar.activation(th[q0 % 2], ps_h[q0 % 2], ACT.Tanh, scale=0.5).then_inc(o.t, 1)

                def out_rows(r, i, k):
                    q0 = r * PAIRS + k
                    act.wait_ge(o.used, RING + SHARED + UNROLL * i + q0 + 1)
                    act.wait_ge(o.ys[q0 % 2], 16 * (UNROLL // 2 * i + q0 // 2 + 1))
                    nc.scalar.activation(ysb[q0 % 2].rearrange("p t d -> p (t d)"),
                                         ps_y[q0 % 2][:, 0:2 * D], ACT.Copy).then_inc(o.ye, 1)

                def store(r, i, k):
                    q0 = r * PAIRS + k
                    act.wait_ge(o.ye, 2 + UNROLL * i + q0 + 1)
                    rows = sorted_y[r].rearrange("(j t p) d -> j p t d", p=P, t=2)
                    act.dma_start(rows[bass.ds(UNROLL * i + k, 1)].rearrange("j p t d -> (j p) t d"),
                                  ysb[q0 % 2][:, :, :]).then_inc(o.ys[q0 % 2], 16)

                for r in range(GROUPS):
                    bring(r, 0, 0)
                    bring(r, 0, 1)
                    pair_tanh(r, 0, 0)
                    bring(r, 0, 2)
                    with act.Fori(0, LOOPS[r]) as i:
                        for k in range(UNROLL):
                            pair_tanh(r, i, k + 1)
                            out_rows(r, i, k)
                            bring(r, i, k + 3)
                            store(r, i, k)
                    for k in range(UNROLL * LOOPS[r], PAIRS):
                        if k + 1 < PAIRS:
                            pair_tanh(r, 0, k + 1)
                        out_rows(r, 0, k)
                        if k + 3 < PAIRS:
                            bring(r, 0, k + 3)
                        store(r, 0, k)
                        if (r, k) == (GROUPS - 1, PAIRS - 2):
                            transposed(f, CHUNKS)
                        if prologue and r == GROUPS - 1 and k in PROLOGUE_PAIRS:
                            use(None, 0, PROLOGUE_PAIRS.index(k), START[PROLOGUE_PAIRS.index(k)][3])

                for m in range(SHARED):
                    if m % NH == 1 and m // NH + 1 < GC:
                        transposed(f, CHUNKS + m // NH + 1)
                    tanh(LATE + m)
                    if prologue and m < PROLOGUE_LATE:
                        i = len(PROLOGUE_PAIRS) + m
                        use(None, 0, i, START[i][3])

            def use(b, base, i, name):
                if name[:-1] not in ("xn", "q", "k", "v", "att"):
                    return
                j = int(name[-1])
                cols = slice(j * 512, (j + 1) * 512)
                act.wait_ge(s_use, base + i + 1)
                if name[:-1] == "q" and b is not None:
                    act.wait_ge(s_parts, 2 * b + 2)
                if name == "v0" and b is not None:
                    act.wait_ge(s_va, BT * b + BT)
                if name[:-1] == "xn":
                    ins = nc.scalar.activation(xnT[:, cols], ps_m, ACT.Copy)
                elif name[:-1] == "q":
                    ins = nc.scalar.activation(qf[:, cols], ps_m, ACT.Copy, scale=DH ** -0.5)
                elif name[:-1] == "k":
                    ins = nc.scalar.activation(kf[:, cols], ps_m, ACT.Copy)
                elif name[:-1] == "v":
                    ins = nc.scalar.activation(vst[:, 4 * j:4 * j + 4, :].rearrange("p t d -> p (t d)"),
                                               ps_m, ACT.Copy)
                else:
                    ins = nc.scalar.activation(attT[:, cols], ps_m, ACT.Copy)
                ins.then_inc(s_free, 1)

            def output(u, ih):
                act.wait_ge(s_pv, 2 + u * NS + LAST_OF_HALF[ih] + 1)
                nc.scalar.activation(oT[ih][:, :], ps_o, ACT.Copy).then_inc(s_ot, 1)

            def steps(b0, span, uses):
                base = len(START) + b0 * len(USES)
                before = []
                for db, g, s in span:
                    b = b0 + db
                    u = b * UNITS + g
                    jt, i0, w, ih = STEPS[s]
                    for pair in range(2):
                        n = u * 2 * NS + 2 * s + pair
                        act.wait_ge(s_s, n + 1)
                        if pair == 0:
                            act.wait_ge(s_pv, u * NS + s + 1)
                        nc.scalar.activation(pT[s % 2][pair][:, :, 0:w], ps_s[pair][:, :, 0:w],
                                             ACT.Exp).then_inc(s_e, 1)
                        if pair == 1:
                            if s == LAST_OF_HALF[0] + 1:
                                output(u, 0)
                            if s == 0 and (g or not isinstance(b, int) or b):
                                output(u - 1, 1)
                        if pair == 0:
                            for i, name in before:
                                use(b0, base, i, name)
                    before = numbered(uses, g, s, db)
                for i, name in before:
                    use(b0, base, i, name)

            for c in range(GC):
                transposed(0, c)
            run_ffn(0, True)
            steps(0, FIRST_STEPS, [])
            with act.Fori(0, BATCH - 1) as b:
                steps(b, BODY_STEPS, USES)
            steps(BATCH - 1, LAST_STEPS, USES_LAST)
            output(BATCH * UNITS - 1, 1)
            for i, (_, _, _, name) in enumerate(END):
                use(BATCH - 1, len(START) + (BATCH - 1) * len(USES) + len(USES_LAST), i, name)
                if i < GC:
                    transposed(1, i)
            run_ffn(1)

        @block.vector
        def _(dve):
            for f in range(2):
                dve.drain().then_inc(ffn[f].u, RING)
                dve.drain().then_inc(ffn[f].used, RING)
                dve.drain().then_inc(ffn[f].ye, 2)
                for i in range(2):
                    dve.drain().then_inc(ffn[f].ys[i], 16)
            dve.drain().then_inc(s_free, 1)
            for s in (s_red, s_e, s_pv):
                dve.drain().then_inc(s, 2)
            dve.drain().then_inc(s_ot, 1)

            def scale_weights(experts):
                for e in experts:
                    nc.vector.tensor_scalar(w1s[:, e, :], w1s[:, e, :], rms_cols[:, e:e + 1], None, ALU.mult)
                dve.drain()

            def statistics(t0, n, to):
                for t in range(n):
                    nc.vector.bn_stats(stats[:, to % GT + t, :], xs[:, bass.ds(t0 + t, 1), :])
                dve.drain()
                for t in range(n):
                    nc.vector.bn_aggr(mv[:, to + t, :], stats[:, to % GT + t, :])

            def batch_stats(f, b):
                statistics(b * BT, BT, b * BT)
                dve.drain().then_inc(ffn[f].mv, 1)

            def chunk_normed(f, c):
                b = c * CT // BT
                dve.wait_ge(ffn[f].rr, b + 1 if b < POOLS_BATCH else b)
                for t in range(c * CT, (c + 1) * CT):
                    nc.vector.tensor_scalar(xh_tile(t), xs[:, t, :], mv[:, t, 0:1], rr[:, t:t + 1],
                                            ALU.subtract, ALU.mult)
                dve.drain().then_inc(ffn[f].xh, 1)

            def add_part(f, r, i):
                j, k = i // TOP_K, i % TOP_K
                dve.wait_ge(ffn[f].got[r][j], 16 * TOP_K * BLOCK)
                dve.drain()
                for t in range(BLOCK * j, BLOCK * (j + 1)):
                    rows = xs[:, r * GT + t, :]
                    nc.vector.scalar_tensor_tensor(rows, got[r][:, k, t, :], gates[r][:, k, t:t + 1],
                                                   rows, ALU.mult, ALU.add)
                if k == TOP_K - 1:
                    dve.drain().then_inc(ffn[f].add, 1)

            def run_ffn(f, prologue=False):
                o = ffn[f]

                def by_tile(a):
                    return a.rearrange("p e t -> p t e")

                def choose(r, part):
                    inv = inv_rms[:, r * GT:(r + 1) * GT]
                    if part == 0:
                        dve.wait_ge(o.lg, (r + 1) * GC)
                        nc.vector.tensor_tensor(
                            lg[:, :, :],
                            ps_l.rearrange("p (r t e) -> p r t e", r=GROUPS, t=GT)[:, r, :, 0:E_ROUTED],
                            inv.unsqueeze(2).to_broadcast([P, GT, E_ROUTED]), ALU.mult)
                        dve.drain()
                        for t in range(GT // 2):
                            nc.vector.max(mx8[:, t, :], lg[:, t, :])
                    if part == 1:
                        for t in range(GT // 2, GT):
                            nc.vector.max(mx8[:, t, :], lg[:, t, :])
                        dve.drain()
                        nc.vector.tensor_tensor(below[:, :, 0:E_ROUTED], lg[:, :, :],
                                                mx8[:, :, 0:1].to_broadcast([P, GT, E_ROUTED]), ALU.subtract)
                        nc.vector.tensor_tensor(below[:, :, E_ROUTED:E_ROUTED + 1], mx8[:, :, 1:2],
                                                mx8[:, :, 0:1], ALU.subtract)
                        dve.drain().then_inc(o.lgs, 1)
                    if part == 2:
                        for t in range(GT // 2):
                            nc.vector.max_index(ix8[:, t, :], mx8[:, t, :], lg[:, t, :])
                    if part == 3:
                        for t in range(GT // 2, GT):
                            nc.vector.max_index(ix8[:, t, :], mx8[:, t, :], lg[:, t, :])
                    if part == 4:
                        dve.drain()
                        nc.vector.tensor_copy(ixf[:, :, :], ix8[:, :, 0:TOP_K])
                        dve.drain()
                        for j in range(TOP_K):
                            nc.vector.tensor_tensor(
                                hot[:, j, :, :], experts_row[:, :].unsqueeze(1).to_broadcast([P, GT, E_ROUTED]),
                                ixf[:, :, j:j + 1].to_broadcast([P, GT, E_ROUTED]), ALU.is_equal)
                        dve.drain()
                        nc.vector.tensor_tensor(by_tile(chosen[:, :, :]), hot[:, 0, :, :], hot[:, 1, :, :],
                                                ALU.add)
                        dve.drain().then_inc(o.cho, 1)

                def flat(a):
                    return a[:, :, :].rearrange("p e t -> p (e t)")

                def place(r, part):
                    of_tile = ps_r[:, 256:256 + E_ROUTED * GT]
                    before = ps_r[:, 0:E_ROUTED * GT]
                    if part == 0:
                        dve.wait_ge(o.cnt, r + 1)
                        nc.vector.tensor_tensor_scan(flat(seen), flat(go_on), of_tile, 0.0, ALU.mult, ALU.add)
                        dve.drain()
                        nc.vector.tensor_tensor(flat(rank), flat(seen), of_tile, ALU.subtract)
                        nc.vector.tensor_tensor(
                            more_than[:, :, :], seen[:, :, GT - 1:GT].to_broadcast([P, E_ROUTED, GT]),
                            hundreds[:, :].unsqueeze(1).to_broadcast([P, E_ROUTED, GT]), ALU.is_gt)
                        dve.drain()
                    if part == 1:
                        nc.vector.tensor_tensor(flat(rank), flat(rank), before, ALU.add)
                        nc.vector.tensor_reduce(ntiles[:, :], more_than[:, :, :], axis=AXX, op=ALU.add)
                        dve.drain()
                        nc.vector.tensor_tensor_scan(ends[:, :], ones_e[:, :], ntiles[:, :], 0.0,
                                                     ALU.mult, ALU.add)
                        dve.drain()
                        nc.vector.tensor_tensor(base_row[:, :], ends[:, :], ntiles[:, :], ALU.subtract)
                        nc.vector.tensor_tensor(
                            ended[:, :, :], ends[0:1, :].unsqueeze(1).to_broadcast([1, RTILES, E_ROUTED]),
                            tiles_row[:, :].unsqueeze(2).to_broadcast([1, RTILES, E_ROUTED]), ALU.is_le)
                        dve.drain()
                    if part == 2:
                        nc.vector.scalar_tensor_tensor(
                            rank[:, :, :], base_row[:, :].unsqueeze(2).to_broadcast([P, E_ROUTED, GT]), float(P),
                            rank[:, :, :], ALU.mult, ALU.add)
                        nc.vector.tensor_reduce(tile_ef[:, :], ended[:, :, :], axis=AXX, op=ALU.add)
                        dve.drain()
                        nc.vector.tensor_scalar(tile_ef[:, :], tile_ef[:, :], float(E_ROUTED - 1), None,
                                                ALU.min)
                        for j in range(TOP_K):
                            nc.vector.tensor_tensor(picked[:, j, :, :], hot[:, j, :, :],
                                                    by_tile(rank[:, :, :]), ALU.mult)
                        dve.drain()
                    if part == 3:
                        both = tile_ef[:, :].rearrange("o (q a) -> o q a", a=2)
                        nc.vector.scalar_tensor_tensor(pair_e[r][:, :], both[:, :, 1], float(EXPERTS),
                                                       both[:, :, 0], ALU.mult, ALU.add)
                        nc.vector.tensor_reduce(posf[:, :, :], picked[:, :, :, :], axis=AXX, op=ALU.add)
                        dve.drain()
                        nc.vector.tensor_copy(pos[r][:, :, :], posf[:, :, :])
                        dve.drain().then_inc(o.pos, 1)
                    if part == 4:
                        dve.wait_ge(o.ex, r + 1)
                        nc.vector.tensor_reduce(esum[:, :], ex[:, :, 0:E_ROUTED], axis=AXX, op=ALU.add)
                        dve.drain()
                        nc.vector.scalar_tensor_tensor(esum[:, :], esum[:, :], GATE_EPS,
                                                       ex[:, :, E_ROUTED], ALU.mult, ALU.add)
                        dve.drain()
                        nc.vector.tensor_scalar(esum[:, :], esum[:, :], 1.0, 4.0, ALU.add, ALU.mult)
                        dve.drain()
                        nc.vector.reciprocal(gates[r][:, 0, :], esum[:, :])
                        dve.drain()
                        nc.vector.tensor_tensor(gates[r][:, 1, :], gates[r][:, 0, :], ex[:, :, E_ROUTED],
                                                ALU.mult)

                def activations(n, slot):
                    dve.wait_ge(o.t, n + 1)
                    nc.vector.scalar_tensor_tensor(uu[slot], th[slot], 1.0, ps_h[slot],
                                                   ALU.add, ALU.mult).then_inc(o.u, 1)

                def add_shared(c, n):
                    dve.drain()
                    dve.wait_ge(o.used, RING + n)
                    rows = xs[:, c * CT:(c + 1) * CT, :]
                    nc.vector.scalar_tensor_tensor(rows, ps_y[0].rearrange("p (t d) -> p t d", t=CT), 0.25,
                                                   rows, ALU.mult, ALU.add).then_inc(o.acc, 1)

                def shared_activations(n):
                    dve.wait_ge(o.used, n + 1)
                    activations(n, n % RING)

                for part in range(5):
                    choose(0, part)
                for part in range(5):
                    place(0, part)
                for c in range(POOLS_CHUNKS.stop, CHUNKS):
                    chunk_normed(f, c)
                for n in range(SHARED):
                    if n in CHOOSE_AT:
                        choose(1, CHOOSE_AT.index(n))
                    if n in PLACE_AT:
                        place(1, PLACE_AT.index(n))
                    shared_activations(n)
                    if n % NH == 1 and n >= NH:
                        add_shared(n // NH - 1, (n // NH) * NH)
                add_shared(GC - 1, SHARED)
                if f == 0:
                    dve.wait_ge(s_wrt, 48)
                    scale_weights(range(E_ROUTED))

                def pair_weights(r, i, k):
                    q0 = r * PAIRS + k
                    both = dve.value_load(pair_e[r][0:1, bass.ds(UNROLL * i + k, 1)],
                                          min_val=0, max_val=EXPERTS * E_ROUTED - 1)
                    es = both % EXPERTS, both // EXPERTS
                    dve.wait_ge(o.used, RING + SHARED + UNROLL * i + q0 - UNROLL + 1)
                    for a in range(2):
                        last = nc.vector.tensor_copy(w12c[q0 % UNROLL][:, a:a + 1, :],
                                                     w12[:, bass.ds(es[a], 1), :])
                    last.then_inc(o.w1, 1)

                def pair_activations(r, i, k):
                    q0 = r * PAIRS + k
                    dve.wait_ge(o.used, RING + SHARED + UNROLL * i + q0 - 1)
                    activations(SHARED + UNROLL * i + q0, q0 % 2)

                for r in range(GROUPS):
                    for k in range(UNROLL - 1):
                        pair_weights(r, 0, k)
                    with dve.Fori(0, LOOPS[r]) as i:
                        for k in range(UNROLL):
                            pair_activations(r, i, k)
                            pair_weights(r, i, k + UNROLL - 1)
                    for k in range(UNROLL * LOOPS[r], PAIRS):
                        pair_activations(r, 0, k)
                        if k + UNROLL - 1 < PAIRS:
                            pair_weights(r, 0, k + UNROLL - 1)
                        if r == GROUPS - 1:
                            for i in range(TOP_K * BLOCKS):
                                if ADD_AT[i] == k:
                                    add_part(f, 0, i)
                        if prologue and r == GROUPS - 1 and k in STATS_PAIRS:
                            at = STATS_PAIRS.index(k) * BT // len(STATS_PAIRS)
                            statistics(at, BT // len(STATS_PAIRS), at)
                            if k == STATS_PAIRS[-1]:
                                dve.drain().then_inc(s_mv, 1)
                        if prologue and r == GROUPS - 1 and k == NORMED_AT:
                            normed(0)
                for m in range(SHARED):
                    shared_activations(LATE + m)
                    if m % NH == 1 and m >= NH:
                        add_shared(GC + m // NH - 1, LATE + m // NH * NH)
                    if prologue:
                        for kind, first in (("q", Q_PARTS_FROM), ("k", K_PARTS_FROM)):
                            if first <= m < first + 4:
                                first_parts(kind, m - first)
                    for i in range(len(LATE_ADD_AT)):
                        if f and m == LATE_ADD_AT[i]:
                            add_part(f, 1, i)
                add_shared(CHUNKS - 1, LATE + SHARED)
                if f:
                    for i in range(len(LATE_ADD_AT), TOP_K * BLOCKS):
                        add_part(f, 1, i)

            def normed(b, first=0, n=BT):
                if first == 0:
                    dve.wait_ge(s_rr, b + 1)
                for t in range(first, first + n):
                    nc.vector.tensor_scalar(xn[:, t, :], xs[:, bass.ds(b * BT + t, 1), :],
                                            mv[:, t, 0:1], rstd[:, t:t + 1], ALU.subtract, ALU.mult)
                if first + n == BT:
                    dve.drain().then_inc(s_xn, 1)

            def reduce_bank(u, parity, n):
                pieces, half = BANKS[n]
                h0, it, _, w = pieces[0]
                dst = (nmax1[:, h0:h0 + len(pieces), it - 4] if half
                       else nmax[parity][:, h0:h0 + len(pieces), it])
                dve.wait_ge(s_b1, u * NB + n + 1)
                nc.vector.tensor_reduce(
                    dst, ps_1[n % 2][:, 0:len(pieces) * w].rearrange("p (h j) -> p h j", j=w),
                    axis=AXX, op=ALU.max, negate=True).then_inc(s_red, 1)

            def join_maxima(parity):
                m = nmax[parity]
                dve.drain()
                nc.vector.tensor_tensor(m[:, :, 4:8], m[:, :, 4:8], nmax1[:, :, :], ALU.min)
                dve.drain().then_inc(s_max, 1)

            def use(b, base, i, g, name, u_next):
                if name[:-1] not in ("o", "proj") and name != "max":
                    return
                dve.wait_ge(s_use, base + i + 1)
                if name == "max":
                    if u_next is not None:
                        dve.wait_ge(s_mw, 16 * u_next)
                    m = ps_m[0:GH * BT, 0:P]
                    nc.vector.tensor_copy(mp[:, 0, :], m)
                    dve.drain()
                    nc.vector.tensor_tensor(mrest[:, :], m, mp[:, 0, :], ALU.subtract).then_inc(s_free, 1)
                    dve.drain()
                    nc.vector.tensor_copy(mp[:, 1, :], mrest[:, :])
                    dve.drain()
                    nc.vector.tensor_tensor(mp[:, 2, :], mrest[:, :], mp[:, 1, :], ALU.subtract
                                            ).then_inc(s_mp, 1)
                elif name[0] == "o":
                    ih = int(name[1])
                    gg = g if ih == 0 else (g - 1) % UNITS
                    v = ps_m.rearrange("p (t h c) -> p t h c", t=4, h=GH)
                    nc.vector.reciprocal(rden[:, :, :], v[:, :, :, DH])
                    dve.drain()
                    nc.vector.tensor_tensor(
                        att[:, 4 * ih:4 * ih + 4, gg * GH * DH:(gg + 1) * GH * DH
                            ].rearrange("p t (h d) -> p t h d", d=DH),
                        v[:, :, :, 0:DH], rden[:, :, :].unsqueeze(3).to_broadcast([P, 4, GH, DH]),
                        ALU.mult).then_inc(s_free, 1)
                else:
                    rows = xs[:, bass.ds(b * BT + 4 * int(name[-1]), 4), :]
                    nc.vector.tensor_tensor(rows, ps_m.rearrange("p (t d) -> p t d", t=4), rows,
                                            ALU.add).then_inc(s_free, 1)

            def first_parts(kind, part):
                src, parts = (qf, qp) if kind == "q" else (kf, kp)
                if part == 0:
                    if kind == "q":
                        dve.wait_ge(s_alw, 16)
                    dve.wait_ge(s_free, [u[3] for u in START].index(kind + "1") + 2)
                    nc.vector.tensor_copy(parts[:, 0, :], src[:, :])
                if part == 1:
                    nc.vector.tensor_tensor(rest[:, :], src[:, :], parts[:, 0, :], ALU.subtract)
                if part == 2:
                    nc.vector.tensor_copy(parts[:, 1, :], rest[:, :])
                if part == 3:
                    nc.vector.tensor_tensor(parts[:, 2, :], rest[:, :], parts[:, 1, :], ALU.subtract)
                    dve.drain().then_inc(s_parts, 1)
                else:
                    dve.drain()

            def steps(b0, span, uses, last=False):
                base = len(START) + b0 * len(USES)
                before = []
                for db, g, s in span:
                    b = b0 + db
                    u = b * UNITS + g
                    banks_now, ahead = banks_at(s)
                    if last and g + ahead >= UNITS:
                        banks_now = []
                    for n in banks_now:
                        reduce_bank(u + ahead, (g + ahead) % 2, n)
                    if s == AHEAD - 1 and len(banks_now):
                        join_maxima((g + 1) % 2)
                    for i, name in numbered(uses, g, s, db):
                        use(b0, base, i, g, name, u + 1)
                    if g == 0 and s in STATS_AT and not last:
                        at = STATS_AT.index(s) * NORM_TILES
                        statistics((b + 1) * BT + at, NORM_TILES, at)
                        if s == STATS_AT[-1]:
                            dve.drain().then_inc(s_mv, 1)
                    if g == 1 and s < len(NORMED_IN) and not last:
                        normed(b + 1, sum(NORMED_IN[:s]), NORMED_IN[s])
                    for i in range(TOP_K * BLOCKS):
                        if not uses and s == STEPS_ADD_AT[i]:
                            add_part(0, 1, i)
                    if last and g == 1 and s == 0:
                        batch_stats(1, 0)
                        batch_stats(1, 1)
                    if last and g == 2 and s < GC:
                        if s == 0:
                            dve.wait_ge(s_parts, 2 * BATCH)
                            dve.wait_ge(s_va, BT * BATCH)
                        chunk_normed(1, s)
                    if last and g == 3 and s == 0:
                        batch_stats(1, 2)
                for args in before:
                    use(*args)

            for b in range(GT // BT):
                dve.wait_ge(s_x[b], 16)
                batch_stats(0, b)
            dve.wait_ge(s_rmsT, 1)
            dve.wait_ge(s_wsh, 16 * 6)
            nc.vector.tensor_copy(rms_cols[:, :], ps_t[0][:, 0:EXPERTS])
            dve.drain()
            scale_weights(range(E_ROUTED, EXPERTS))
            dve.drain().then_inc(s_wready, 1)
            for c in range(GC):
                chunk_normed(0, c)
            for b in range(GT // BT, BATCH):
                dve.wait_ge(s_x[b], 16)
                batch_stats(0, b)
            dve.wait_ge(s_c, 1)
            run_ffn(0, True)
            nc.vector.memset(ps_o, 0.0).then_inc(s_oz, 1)
            for n in range(NB):
                reduce_bank(0, 0, n)
            join_maxima(0)
            use(0, 0, len(START) - 1, 0, "max", None)
            for n in range(EARLY):
                reduce_bank(1, 1, n)
            steps(0, FIRST_STEPS, [])
            with dve.Fori(0, BATCH - 1) as b:
                steps(b, BODY_STEPS, USES)
            steps(BATCH - 1, LAST_STEPS, USES_LAST, True)
            for i, (_, _, _, name) in enumerate(END):
                use(BATCH - 1, len(START) + (BATCH - 1) * len(USES) + len(USES_LAST), i, 0, name, None)
            dve.drain()
            batch_stats(1, BATCH - 1)
            run_ffn(1)

        @block.tensor
        def _(pe):
            mm = nc.tensor.matmul
            pe.wait_ge(s_id, 1)
            pe.wait_ge(s_wsh, 16 * 6)
            nc.tensor.transpose(ps_t[0][:, 0:EXPERTS], rms_rows[:, :], ident[0:EXPERTS, 0:EXPERTS]
                                ).then_inc(s_rmsT, 1)
            pe.wait_ge(s_wready, 1)

            def transposes(f, i):
                o = ffn[f]
                c = i if i < CHUNKS else i - GC
                if c in POOLS_CHUNKS:
                    pe.wait_ge(o.xh2, c - POOLS_CHUNKS.start + 1)
                else:
                    pe.wait_ge(o.xh, c + 1 if c < POOLS_CHUNKS.start else c + 1 - len(POOLS_CHUNKS))
                if i >= 2:
                    pe.wait_ge(o.xts, i - 1 if i < CHUNKS else i)
                for t in range(CT):
                    last = nc.tensor.transpose(ps_t[i % 2 if i < CHUNKS else 0][:, t * P:(t + 1) * P],
                                               xh_tile(c * CT + t), ident[:, :])
                last.then_inc(o.xt, 1)

            def logits(f, c):
                pe.wait_ge(ffn[f].xts, c + 1)
                if c == GC:
                    pe.wait_ge(ffn[f].lgs, 1)
                for t in range(CT):
                    at = (c * CT + t) * RS
                    last = mm(ps_l[:, at:at + E_ROUTED], xT[c][:, t * P:(t + 1) * P],
                              wr[:, :], start=True, stop=True)
                last.then_inc(ffn[f].lg, 1)

            def head(f):
                transposes(f, 0)
                for c in range(GC):
                    if c + 1 < GC:
                        transposes(f, c + 1)
                    logits(f, c)

            def run_ffn(f, prologue=False):
                o = ffn[f]

                def hidden(n, x_from):
                    pe.wait_ge(o.u, n + 1)
                    e, half = HALVES[(n if n < SHARED else n - LATE) % NH]
                    mm(ps_h[n % RING], w1s[:, e, half * P:(half + 1) * P], x_from,
                       start=True, stop=True).then_inc(o.h, 1)

                def product(n):
                    m = n if n < SHARED else n - LATE + SHARED
                    c, (e, half) = m // NH, HALVES[m % NH]
                    if m % NH == 0 and c:
                        pe.wait_ge(o.acc, c)
                    if n == LATE:
                        pe.wait_ge(o.ye, 2 + ROUTED - 1)
                    pe.wait_ge(o.u, RING + n + 1)
                    for t in range(CT):
                        last = mm(ps_y[0][:, t * D:(t + 1) * D],
                                  uu[n % RING][:, t * P:(t + 1) * P], w2s[:, e, half, :],
                                  start=(m % NH == 0 and t == 0), stop=(m % NH == NH - 1),
                                  skip_group_check=True)
                    last.then_inc(o.used, 1)

                def ranks(r):
                    pe.wait_ge(o.cho, r + 1)
                    if r:
                        pe.wait_ge(o.pos, r)
                    c = chosen[:, :, :].rearrange("p e t -> p (e t)")
                    w = E_ROUTED * GT
                    mm(ps_r[:, 0:w], tri[:, :], c, start=True, stop=True)
                    mm(ps_r[:, 256:256 + w], onesb[:, :], c, start=True, stop=True).then_inc(o.cnt, 1)

                pe.wait_ge(s_c, 1)
                for c in range(GC, CHUNKS):
                    if c == RANKS_CHUNK[f]:
                        ranks(0)
                    transposes(f, c)
                    if c > GC:
                        logits(f, c - 1)
                logits(f, CHUNKS - 1)
                if f == 0:
                    pe.wait_ge(s_wready, 1)
                hidden(0, xT[0])
                hidden(1, xT[0])
                for n in range(SHARED):
                    if n + 2 < SHARED:
                        hidden(n + 2, xT[(n + 2) // NH])
                    product(n)
                    if n == RANKS_AT:
                        ranks(1)

                def pair_transposes(r, i, k):
                    q0 = r * PAIRS + k
                    pe.wait_ge(o.xl[q0 % 2], 16 * (UNROLL // 2 * i + q0 // 2 + 1))
                    if k >= 2 or r:
                        pe.wait_ge(o.pe, UNROLL * i + q0 - 1)
                    for t in range(2):
                        last = nc.tensor.transpose(ps_tp[q0 % 2][:, t * P:(t + 1) * P], xld[q0 % 2][:, t, :],
                                                   ident[:, :])
                    last.then_inc(o.pt, 1)

                def pair_hidden(r, i, k):
                    q0 = r * PAIRS + k
                    pe.wait_ge(o.pe, UNROLL * i + q0 + 1)
                    pe.wait_ge(o.w1, UNROLL * i + q0 + 1)
                    pe.wait_ge(o.u, RING + SHARED + UNROLL * i + q0 - 1)
                    for half in range(2):
                        for a in range(2):
                            at = (2 * half + a) * P
                            last = mm(ps_h[q0 % 2][:, at:at + P],
                                      w12c[q0 % UNROLL][:, a, half * P:(half + 1) * P],
                                      xTp[q0 % 2][:, a * P:(a + 1) * P], start=True, stop=True)
                    last.then_inc(o.h, 1)

                def pair_products(r, i, k):
                    q0 = r * PAIRS + k
                    pe.wait_ge(o.ye, UNROLL * i + q0 + 1)
                    pe.wait_ge(o.u, RING + SHARED + UNROLL * i + q0 + 1)
                    for a in range(2):
                        for half in range(2):
                            at = (2 * half + a) * P
                            last = mm(ps_y[q0 % 2][:, a * D:(a + 1) * D], uu[q0 % 2][:, at:at + P],
                                      w12c[q0 % UNROLL][:, a, HID + half * D:HID + (half + 1) * D],
                                      start=(half == 0), stop=(half == 1))
                    last.then_inc(o.used, 1)

                if prologue:
                    pe.wait_ge(s_wat, 32)
                pe.wait_ge(o.pos, GROUPS)
                pe.wait_ge(o.u, RING + SHARED)
                pe.wait_ge(o.acc, GC)
                for r in range(GROUPS):
                    pair_transposes(r, 0, 0)
                    pair_transposes(r, 0, 1)
                    pair_hidden(r, 0, 0)
                    with pe.Fori(0, LOOPS[r]) as i:
                        for k in range(UNROLL):
                            pair_transposes(r, i, k + 2)
                            pair_hidden(r, i, k + 1)
                            pair_products(r, i, k)
                    for k in range(UNROLL * LOOPS[r], PAIRS):
                        if k + 2 < PAIRS:
                            pair_transposes(r, 0, k + 2)
                        if k + 1 < PAIRS:
                            pair_hidden(r, 0, k + 1)
                        elif r == GROUPS - 1:
                            pe.wait_ge(o.xts, CHUNKS + 1)
                            hidden(LATE, xT[0])
                            hidden(LATE + 1, xT[0])
                        pair_products(r, 0, k)
                        if (r, k) == (GROUPS - 1, PAIRS - 2):
                            transposes(f, CHUNKS)
                        if prologue and r == GROUPS - 1 and k in PROLOGUE_PAIRS:
                            use(0, 0, PROLOGUE_PAIRS.index(k), START[PROLOGUE_PAIRS.index(k)][3], 0, 0)
                for m in range(SHARED):
                    if m % NH == 0 and m // NH + 1 < GC:
                        transposes(f, CHUNKS + m // NH + 1)
                    if prologue and m < PROLOGUE_LATE:
                        i = len(PROLOGUE_PAIRS) + m
                        use(0, 0, i, START[i][3], 0, 0)
                    if m + 2 < SHARED:
                        if (m + 2) % NH == 0:
                            pe.wait_ge(o.xts, CHUNKS + (m + 2) // NH + 1)
                        hidden(LATE + m + 2, xT[(m + 2) // NH % 2])
                    product(LATE + m)

            def first_pass(u, b, g, n):
                pieces, half = BANKS[n]
                if n == 0:
                    pe.wait_ge(s_rows[g], 16 * 2 * PARTS * (b + 1))
                    if g == UNITS - 1:
                        pe.wait_ge(s_alr, 16 * (UNITS + 2))
                pe.wait_ge(s_red, u * NB + n + 1)
                for j, (h, it, j0, w) in enumerate(pieces):
                    dst = ps_1[n % 2][:, j * w:(j + 1) * w]
                    diagonal = j0 + w == (it + 1) * P
                    last = mm(dst, qs[g][0:PASS1_ROWS, h, it * P:(it + 1) * P],
                              ks[g][0:PASS1_ROWS, h, j0:j0 + w], start=True, stop=not diagonal)
                    if diagonal:
                        last = mm(dst[:, w - P:w], identb[:, :], maskb[:, :], start=False, stop=True)
                last.then_inc(s_b1, 1)

            def scores(u, g, s, pair):
                jt, i0, w, ih = STEPS[s]
                pe.wait_ge(s_e, u * 2 * NS + 2 * s + pair + 1)
                for j in range(2):
                    h = 2 * pair + j
                    diagonal = i0 == jt * P
                    last = mm(ps_s[pair][:, j, 0:w], ks[g][:, h, jt * P:(jt + 1) * P],
                              qs[g][:, h, i0:i0 + w], start=True, stop=not diagonal)
                    if diagonal:
                        last = mm(ps_s[pair][:, j, 0:P], maskb[:, :], identb[:, :], start=False, stop=True)
                last.then_inc(s_s, 1)

            def weigh(u, b, g, s):
                jt, i0, w, ih = STEPS[s]
                if jt == 0:
                    pe.wait_ge(s_ot, 2 * u + ih + 1)
                if g == 0 and s <= LAST_OF_HALF[0] or g == 0 and jt > LAST_OF_HALF[0]:
                    pe.wait_ge(s_va, BT * b + jt + 1)
                pe.wait_ge(s_e, 2 + u * 2 * NS + 2 * s + 2)
                for h in range(GH):
                    last = mm(ps_o[32 * h:32 * h + VW, i0 - HALF * ih:HALF],
                              vaug[:, jt, g * GH + h, :], pT[s % 2][h // 2][:, h % 2, 0:w],
                              start=(jt == 0), stop=(s == LAST_OF_HALF[ih]))
                last.then_inc(s_pv, 1)

            def use(b, base, i, name, u, g):
                kind, j = (name, 0) if name == "max" else (name[:-1], int(name[-1]))
                cols = slice(512 * j, 512 * (j + 1))
                if kind == "xn" and j == 0:
                    pe.wait_ge(s_xn, b + 1)
                if kind == "max":
                    pe.wait_ge(s_max, u + 1)
                if kind == "o":
                    pe.wait_ge(s_ot, 1 + 2 * u + j + 1)
                pe.wait_ge(s_free, base + i + 1)
                if kind in ("xn", "att"):
                    src = xn if kind == "xn" else att
                    for t in range(4):
                        last = nc.tensor.transpose(ps_m[:, t * P:(t + 1) * P], src[:, 4 * j + t, :],
                                                   ident[:, :])
                elif kind in ("q", "k"):
                    at = 0 if kind == "q" else D
                    last = mm(ps_m, wqkv[:, at:at + D], xnT[:, cols], start=True, stop=True)
                elif kind in ("v", "proj"):
                    src, w = (xnT, wqkv[:, 2 * D:]) if kind == "v" else (attT, wproj[:, :])
                    for t in range(4):
                        last = mm(ps_m[:, t * D:(t + 1) * D], src[:, (4 * j + t) * P:(4 * j + t + 1) * P], w,
                                  start=True, stop=True)
                elif kind == "max":
                    last = nc.tensor.transpose(ps_m[0:GH * BT, 0:P],
                                               nmax[g % 2][:, :, :].rearrange("p h t -> p (h t)"), ident[:, :])
                else:
                    for t in range(4):
                        last = nc.tensor.transpose(ps_m[:, t * P:(t + 1) * P], oT[j][:, t * P:(t + 1) * P],
                                                   ident[:, :])
                last.then_inc(s_use, 1)

            def steps(b0, span, uses, last=False):
                base = len(START) + b0 * len(USES)
                for db, g, s in span:
                    b = b0 + db
                    u = b * UNITS + g
                    s1, g1 = (s + 1, g) if s + 1 < NS else (0, (g + 1) % UNITS)
                    u1 = u if s + 1 < NS else u + 1
                    more = not (last and g == UNITS - 1 and s == NS - 1)
                    todo, ahead = banks_at(s)
                    if last and g + ahead >= UNITS:
                        todo = []
                    gb, bb = (g + ahead) % UNITS, b + (g + ahead) // UNITS
                    for n in todo[0:1]:
                        first_pass(u + ahead, bb, gb, n)
                    if more and s1 == 0:
                        pe.wait_ge(s_mrow, 16 * (u1 + 1))
                    if more:
                        scores(u1, g1, s1, 0)
                    for n in todo[1:2]:
                        first_pass(u + ahead, bb, gb, n)
                    if more:
                        scores(u1, g1, s1, 1)
                    for n in todo[2:3]:
                        first_pass(u + ahead, bb, gb, n)
                    for i, name in numbered(uses, g, s, db):
                        if name == "max":
                            use(0, base, i, name, u + 1, g + 1)
                        elif name in ("o0", "o1"):
                            use(0, base, i, name, u if name == "o0" else u - 1, 0)
                        else:
                            use(b + 1, base, i, name, 0, 0)
                    weigh(u, b, g, s)
                    for n in todo[3:]:
                        first_pass(u + ahead, bb, gb, n)

            head(0)
            run_ffn(0, True)
            pe.wait_ge(s_oz, 1)
            pe.wait_ge(s_alr, 16 * (UNITS - 1))
            pe.wait_ge(ffn[0].acc, CHUNKS)
            pe.wait_ge(ffn[0].u, RING + LATE + SHARED)
            for n in range(NB):
                first_pass(0, 0, 0, n)
            use(0, 0, len(START) - 1, "max", 0, 0)
            for n in range(EARLY):
                first_pass(1, 0, 1, n)
            pe.wait_ge(s_mrow, 16)
            scores(0, 0, 0, 0)
            scores(0, 0, 0, 1)
            steps(0, FIRST_STEPS, [])
            with pe.Fori(0, BATCH - 1) as b:
                steps(b, BODY_STEPS, USES)
            steps(BATCH - 1, LAST_STEPS, USES_LAST, True)
            for i, (_, _, _, name) in enumerate(END):
                use(0, len(START) + (BATCH - 1) * len(USES) + len(USES_LAST), i, name,
                    BATCH * UNITS - 1, 0)
                if i == 0:
                    pe.wait_ge(s_red, 2 + BATCH * UNITS * NB)
                    pe.wait_ge(s_e, 2 + 2 * BATCH * UNITS * NS)
                if i < GC:
                    transposes(1, i)
            for c in range(GC):
                logits(1, c)
            run_ffn(1)


def kernel(L0_attn_x, L0_attn_w_qkv, L0_attn_w_proj, L0_ffn_router_w, L0_ffn_rms_w, L0_ffn_w1,
           L0_ffn_w2, L0_ffn_rms_w_s, L0_ffn_w1_s, L0_ffn_w2_s):
    import numpy as np
    import concourse.bacc as bacc
    from concourse.bass_utils import run_bass_kernel_spmd

    start = 2.0 ** (-2.0 ** (-(math.log2(HEADS) - 3)))
    slopes = np.array([start * start ** i for i in range(HEADS)], np.float32)
    alibi = slopes[:, None] * np.arange(SEQ, dtype=np.float32)[None, :]

    nc = bacc.Bacc("TRN2", target_bir_lowering=False, num_devices=1)
    arrays, aps = {}, []
    for name, a in (("x", L0_attn_x), ("w_qkv", L0_attn_w_qkv), ("w_proj", L0_attn_w_proj),
                    ("router_w", L0_ffn_router_w), ("rms_w", L0_ffn_rms_w), ("w1", L0_ffn_w1),
                    ("w2", L0_ffn_w2), ("rms_w_s", L0_ffn_rms_w_s), ("w1_s", L0_ffn_w1_s),
                    ("w2_s", L0_ffn_w2_s), ("alibi", alibi)):
        a = np.ascontiguousarray(a)
        arrays[name] = a
        aps.append(nc.dram_tensor(name, a.shape, mybir.dt.from_np(a.dtype), kind="ExternalInput").ap())
    out = nc.dram_tensor("out", (BATCH, SEQ, D), F32, kind="ExternalOutput").ap()

    def by_tile(a):
        return a.rearrange("b (t p) d -> p (b t) d", p=P)

    build(nc, by_tile(aps[0]), aps[0].rearrange("b n d -> (b n) d"), *aps[1:], by_tile(out))
    r = run_bass_kernel_spmd(nc, [arrays], core_ids=[0])
    return r.results[0]["out"]
```
